# Optimizing a Trainium2 kernel written in Bass

```python
import numpy as np
import jax
import jax.numpy as jnp

def _softmax(x, axis=-1):
    return jax.nn.softmax(x, axis=axis)

def _gelu(x):
    return jax.nn.gelu(x, approximate=True)

def _silu(x):
    return jax.nn.silu(x)

def _sigmoid(x):
    return jax.nn.sigmoid(x)

def _layernorm(x, axis=-1, eps=1e-05):
    m = jnp.mean(x, axis=axis, keepdims=True)
    v = jnp.var(x, axis=axis, keepdims=True)
    return (x - m) / jnp.sqrt(v + eps)

def _scatter_add(tgt, idx, src, axis=0):
    return tgt.at[idx].add(src)

def _segment_sum(src, seg, n):
    return jax.ops.segment_sum(src, seg, n)
kernel_name = 'mk_adj_seq_d2_adj_r2_44786b'

def setup_inputs(seed: int=0):
    np.random.seed(seed)
    _w = jnp.asarray

    def _rec_inputs():
        import jax
        import jax.numpy as jnp
        _gk = jax.random.key(seed)
        x = -0.0005207 + 1.001 * jax.random.normal(jax.random.fold_in(_gk, 1), (2048, 256), jnp.float32)
        _a = jax.random.bernoulli(jax.random.fold_in(_gk, 2), 0.0078125, (2048, 2048))
        _a = jnp.logical_or(_a, jnp.swapaxes(_a, -1, -2))
        _a = jnp.logical_or(_a, jnp.eye(2048, dtype=bool))
        adj = _a.astype(jnp.int32)
        return (x, adj)
    x, adj = _rec_inputs()

    def _L0_gnn_setup():
        import jax, jax.numpy as jnp
        import numpy as np
        D_MODEL = 256
        N_HEADS = 8
        D_K = D_MODEL // N_HEADS
        D_FF = 1024
        N = 2048
        EPS = 1e-05

        def _layer_norm(x, g, b):
            mu = jnp.mean(x, axis=-1, keepdims=True)
            var = jnp.mean(jnp.square(x - mu), axis=-1, keepdims=True)
            return (x - mu) * jax.lax.rsqrt(var + EPS) * g + b
        key = jax.random.key(seed)
        ks = jax.random.split(key, 16)
        s = 1.0 / np.sqrt(D_MODEL)
        sf = 1.0 / np.sqrt(D_FF)
        inp = {'h': jax.random.normal(ks[0], (N, D_MODEL), dtype=jnp.float32), 'adj': jax.random.randint(ks[1], (N, N), 0, 2, dtype=jnp.int32), 'Wq': jax.random.uniform(ks[2], (D_MODEL, D_MODEL), jnp.float32, -s, s), 'bq': jnp.zeros((D_MODEL,), jnp.float32), 'Wk': jax.random.uniform(ks[3], (D_MODEL, D_MODEL), jnp.float32, -s, s), 'bk': jnp.zeros((D_MODEL,), jnp.float32), 'Wv': jax.random.uniform(ks[4], (D_MODEL, D_MODEL), jnp.float32, -s, s), 'bv': jnp.zeros((D_MODEL,), jnp.float32), 'Wo': jax.random.uniform(ks[5], (D_MODEL, D_MODEL), jnp.float32, -s, s), 'bo': jnp.zeros((D_MODEL,), jnp.float32), 'W1': jax.random.uniform(ks[6], (D_FF, D_MODEL), jnp.float32, -s, s), 'b1': jnp.zeros((D_FF,), jnp.float32), 'W2': jax.random.uniform(ks[7], (D_MODEL, D_FF), jnp.float32, -sf, sf), 'b2': jnp.zeros((D_MODEL,), jnp.float32), 'ln1_g': jnp.ones((D_MODEL,), jnp.float32), 'ln1_b': jnp.zeros((D_MODEL,), jnp.float32), 'ln2_g': jnp.ones((D_MODEL,), jnp.float32), 'ln2_b': jnp.zeros((D_MODEL,), jnp.float32)}
        return inp
    _L0_gnn_all = _L0_gnn_setup()
    _L0_gnn_in = {k: v for k, v in _L0_gnn_all.items() if k in ('Wq', 'bq', 'Wk', 'bk', 'Wv', 'bv', 'Wo', 'bo', 'W1', 'b1', 'W2', 'b2', 'ln1_g', 'ln1_b', 'ln2_g', 'ln2_b')}
    del _L0_gnn_all

    def _L1_gnn_setup():
        import jax, jax.numpy as jnp
        import numpy as np
        N, DIM = (2048, 256)
        F_OUT = DIM // 8
        HID = int(DIM * 2.0)
        ALPHA = 0.2
        MASK_VAL = -9000000000000000.0

        def _layernorm(x, g, b, eps=1e-05):
            mu = x.mean(-1, keepdims=True)
            var = ((x - mu) ** 2).mean(-1, keepdims=True)
            return (x - mu) * jax.lax.rsqrt(var + eps) * g + b
        key = jax.random.key(seed)
        ks = jax.random.split(key, 8)
        x = jax.random.normal(ks[0], (N, DIM), jnp.float32)
        adj = jax.random.randint(ks[1], (N, N), 0, 2, jnp.int32)
        W = jax.random.normal(ks[2], (DIM, F_OUT), jnp.float32) * 0.1
        a = jax.random.normal(ks[3], (2 * F_OUT, 1), jnp.float32) * 0.1
        fc_w = jax.random.normal(ks[4], (DIM, F_OUT), jnp.float32) * 0.1
        fc_b = jnp.zeros((DIM,), jnp.float32)
        ln1_g = jnp.ones((DIM,), jnp.float32)
        ln1_b = jnp.zeros((DIM,), jnp.float32)
        ln2_g = jnp.ones((DIM,), jnp.float32)
        ln2_b = jnp.zeros((DIM,), jnp.float32)
        fc1_w = jax.random.normal(ks[5], (HID, DIM), jnp.float32) * 0.05
        fc1_b = jnp.zeros((HID,), jnp.float32)
        fc2_w = jax.random.normal(ks[6], (DIM, HID), jnp.float32) * 0.05
        fc2_b = jnp.zeros((DIM,), jnp.float32)
        return dict(x=x, adj=adj, W=W, a=a, fc_w=fc_w, fc_b=fc_b, ln1_g=ln1_g, ln1_b=ln1_b, ln2_g=ln2_g, ln2_b=ln2_b, fc1_w=fc1_w, fc1_b=fc1_b, fc2_w=fc2_w, fc2_b=fc2_b)
    _L1_gnn_all = _L1_gnn_setup()
    _L1_gnn_in = {k: v for k, v in _L1_gnn_all.items() if k in ('W', 'a', 'fc_w', 'fc_b', 'ln1_g', 'ln1_b', 'ln2_g', 'ln2_b', 'fc1_w', 'fc1_b', 'fc2_w', 'fc2_b')}
    del _L1_gnn_all
    return {'x': x, 'adj': adj, 'L0_gnn_Wq': _L0_gnn_in['Wq'], 'L0_gnn_bq': _L0_gnn_in['bq'], 'L0_gnn_Wk': _L0_gnn_in['Wk'], 'L0_gnn_bk': _L0_gnn_in['bk'], 'L0_gnn_Wv': _L0_gnn_in['Wv'], 'L0_gnn_bv': _L0_gnn_in['bv'], 'L0_gnn_Wo': _L0_gnn_in['Wo'], 'L0_gnn_bo': _L0_gnn_in['bo'], 'L0_gnn_W1': _L0_gnn_in['W1'], 'L0_gnn_b1': _L0_gnn_in['b1'], 'L0_gnn_W2': _L0_gnn_in['W2'], 'L0_gnn_b2': _L0_gnn_in['b2'], 'L0_gnn_ln1_g': _L0_gnn_in['ln1_g'], 'L0_gnn_ln1_b': _L0_gnn_in['ln1_b'], 'L0_gnn_ln2_g': _L0_gnn_in['ln2_g'], 'L0_gnn_ln2_b': _L0_gnn_in['ln2_b'], 'L1_gnn_W': _L1_gnn_in['W'], 'L1_gnn_a': _L1_gnn_in['a'], 'L1_gnn_fc_w': _L1_gnn_in['fc_w'], 'L1_gnn_fc_b': _L1_gnn_in['fc_b'], 'L1_gnn_ln1_g': _L1_gnn_in['ln1_g'], 'L1_gnn_ln1_b': _L1_gnn_in['ln1_b'], 'L1_gnn_ln2_g': _L1_gnn_in['ln2_g'], 'L1_gnn_ln2_b': _L1_gnn_in['ln2_b'], 'L1_gnn_fc1_w': _L1_gnn_in['fc1_w'], 'L1_gnn_fc1_b': _L1_gnn_in['fc1_b'], 'L1_gnn_fc2_w': _L1_gnn_in['fc2_w'], 'L1_gnn_fc2_b': _L1_gnn_in['fc2_b']}

def reference(x, adj, L0_gnn_Wq, L0_gnn_bq, L0_gnn_Wk, L0_gnn_bk, L0_gnn_Wv, L0_gnn_bv, L0_gnn_Wo, L0_gnn_bo, L0_gnn_W1, L0_gnn_b1, L0_gnn_W2, L0_gnn_b2, L0_gnn_ln1_g, L0_gnn_ln1_b, L0_gnn_ln2_g, L0_gnn_ln2_b, L1_gnn_W, L1_gnn_a, L1_gnn_fc_w, L1_gnn_fc_b, L1_gnn_ln1_g, L1_gnn_ln1_b, L1_gnn_ln2_g, L1_gnn_ln2_b, L1_gnn_fc1_w, L1_gnn_fc1_b, L1_gnn_fc2_w, L1_gnn_fc2_b):
    import jax
    import jax.numpy as jnp

    def _L0_gnn_ref(h, adj, Wq, bq, Wk, bk, Wv, bv, Wo, bo, W1, b1, W2, b2, ln1_g, ln1_b, ln2_g, ln2_b):
        import jax, jax.numpy as jnp
        import numpy as np
        D_MODEL = 256
        N_HEADS = 8
        D_K = D_MODEL // N_HEADS
        D_FF = 1024
        N = 2048
        EPS = 1e-05

        def _layer_norm(x, g, b):
            mu = jnp.mean(x, axis=-1, keepdims=True)
            var = jnp.mean(jnp.square(x - mu), axis=-1, keepdims=True)
            return (x - mu) * jax.lax.rsqrt(var + EPS) * g + b
        n = h.shape[0]
        mask = adj.astype(jnp.float32) + jnp.eye(n, dtype=jnp.float32)
        q = (h @ Wq.T + bq).reshape(n, N_HEADS, D_K)
        k = (h @ Wk.T + bk).reshape(n, N_HEADS, D_K)
        v = (h @ Wv.T + bv).reshape(n, N_HEADS, D_K)
        scores = jnp.einsum('nhd,mhd->hnm', q, k) / jnp.sqrt(jnp.float32(D_K))
        scores = jnp.where(mask[None, :, :] == 0, jnp.float32(-1000000000.0), scores)
        attn = jax.nn.softmax(scores, axis=-1)
        ctx = jnp.einsum('hnm,mhd->nhd', attn, v).reshape(n, D_MODEL)
        attn_out = ctx @ Wo.T + bo
        h1 = _layer_norm(h + attn_out, ln1_g, ln1_b)
        ff = jax.nn.relu(h1 @ W1.T + b1) @ W2.T + b2
        h2 = _layer_norm(h1 + ff, ln2_g, ln2_b)
        return h2

    def _L1_gnn_ref(x, adj, W, a, fc_w, fc_b, ln1_g, ln1_b, ln2_g, ln2_b, fc1_w, fc1_b, fc2_w, fc2_b):
        import jax, jax.numpy as jnp
        import numpy as np
        N, DIM = (2048, 256)
        F_OUT = DIM // 8
        HID = int(DIM * 2.0)
        ALPHA = 0.2
        MASK_VAL = -9000000000000000.0

        def _layernorm(x, g, b, eps=1e-05):
            mu = x.mean(-1, keepdims=True)
            var = ((x - mu) ** 2).mean(-1, keepdims=True)
            return (x - mu) * jax.lax.rsqrt(var + eps) * g + b
        h = _layernorm(x, ln1_g, ln1_b)
        Wh = h @ W
        f_src = Wh @ a[:F_OUT, 0]
        f_dst = Wh @ a[F_OUT:, 0]
        e = f_src[:, None] + f_dst[None, :]
        e = jnp.where(e >= 0, e, ALPHA * e)
        att = jax.nn.softmax(jnp.where(adj > 0, e, MASK_VAL), axis=1)
        h_prime = att @ Wh
        attn_out = h_prime @ fc_w.T + fc_b
        x = x + attn_out
        h2 = _layernorm(x, ln2_g, ln2_b)
        m = jax.nn.gelu(h2 @ fc1_w.T + fc1_b, approximate=False)
        m = m @ fc2_w.T + fc2_b
        return x + m
    x = _L0_gnn_ref(x, adj, L0_gnn_Wq, L0_gnn_bq, L0_gnn_Wk, L0_gnn_bk, L0_gnn_Wv, L0_gnn_bv, L0_gnn_Wo, L0_gnn_bo, L0_gnn_W1, L0_gnn_b1, L0_gnn_W2, L0_gnn_b2, L0_gnn_ln1_g, L0_gnn_ln1_b, L0_gnn_ln2_g, L0_gnn_ln2_b)
    x = _L1_gnn_ref(x, adj, L1_gnn_W, L1_gnn_a, L1_gnn_fc_w, L1_gnn_fc_b, L1_gnn_ln1_g, L1_gnn_ln1_b, L1_gnn_ln2_g, L1_gnn_ln2_b, L1_gnn_fc1_w, L1_gnn_fc1_b, L1_gnn_fc2_w, L1_gnn_fc2_b)
    return x

_drawn_inputs = setup_inputs


def setup_inputs(seed=0):
    import zlib

    import numpy as np

    out = dict(_drawn_inputs(seed))
    spreads = {'L0_gnn_bq': (0.0, 0.8),
     'L0_gnn_bk': (0.0, 0.8),
     'L0_gnn_bv': (0.0, 0.1),
     'L0_gnn_bo': (0.0, 0.1),
     'L0_gnn_b1': (0.0, 0.1),
     'L0_gnn_b2': (0.0, 0.1),
     'L0_gnn_ln1_g': (1.0, 0.2),
     'L0_gnn_ln1_b': (0.0, 0.1),
     'L0_gnn_ln2_g': (1.0, 0.2),
     'L0_gnn_ln2_b': (0.0, 0.1),
     'L1_gnn_fc_b': (0.0, 0.1),
     'L1_gnn_ln1_g': (1.0, 0.2),
     'L1_gnn_ln1_b': (0.0, 0.1),
     'L1_gnn_ln2_g': (1.0, 0.2),
     'L1_gnn_ln2_b': (0.0, 0.1),
     'L1_gnn_fc1_b': (0.0, 0.1),
     'L1_gnn_fc2_b': (0.0, 0.1)}
    factors = {'L0_gnn_Wq': 2.749, 'L0_gnn_Wk': 2.696}
    for name, (base, spread) in spreads.items():
        noise = np.random.default_rng([zlib.crc32(name.encode()), seed]).standard_normal(out[name].shape)
        drawn = base * np.exp(spread * noise) if base else spread * noise
        out[name] = jnp.asarray(drawn.astype(out[name].dtype))
    for name, factor in factors.items():
        out[name] = (out[name] * factor).astype(out[name].dtype)
    return out
```

```python
from contextlib import ExitStack

import numpy as np

import concourse.bass as bass
from concourse import mybir

ALU = mybir.AluOpType
ACT = mybir.ActivationFunctionType
F32 = mybir.dt.float32
F16 = mybir.dt.float16
BF16 = mybir.dt.bfloat16
I32 = mybir.dt.int32

P = 128
N, D = 2048, 256
H = 8
DK = D // H
HG = P // DK
G = H // HG
C = D // P
FF = 1024
HID = 512
KC = N // P
QB = 256
NB = N // QB
RB = QB // P
TPB = G * RB * HG
HALF = N // 2
W = 512
PBUF = 4
NEG = -2.0 ** 100
EPS = 1e-5
SCALE = 1.0 / float(np.sqrt(np.float32(DK)))
BIG = 3.0e38
SQ = 512
NS = N // SQ
ST = SQ // P


def wait(eng, sem, value):
    if isinstance(value, int) and value <= 0:
        return
    eng.wait_ge(sem, value)


def holder(eng, sem):
    return lambda: eng.sem_inc(sem, 1)


def tile_of(t):
    return t // (RB * HG), (t % (RB * HG)) // HG, t % HG


def build(nc, a, out):
    x1_dram = nc.dram_tensor("x1_scratch", (N, D), F32, kind="Internal").ap()
    q_dram = nc.dram_tensor("q_scratch", (2, D, N), F16, kind="Internal").ap()

    with ExitStack() as whole:
        def sem(name):
            return whole.enter_context(nc.semaphore(name))

        def sbuf(ctx, name, shape, dt=F32):
            return ctx.enter_context(nc.sbuf_tensor(name, shape, dt))

        sc = whole.enter_context(nc.psum_tensor("score_ps", [P, 2, HALF], F32))
        trp = whole.enter_context(nc.psum_tensor("transpose_ps", [P, 2, W], F32))
        cx = whole.enter_context(nc.psum_tensor("context_ps", [P, W], F32))
        ms = whole.enter_context(nc.psum_tensor("misc_ps", [P, W], F32))

        ident = sbuf(whole, "ident", [P, P])
        mhalf = sbuf(whole, "minus_half", [P, 4])
        whx = sbuf(whole, "whx", [P, KC, DK + 2])

        s_id = sem("s_id")
        s_mh = sem("s_mh")

        with ExitStack() as l0:
            kst = sbuf(l0, "k_stack", [P, H, N], F16)
            v = sbuf(l0, "v", [P, KC, D])
            pb = sbuf(l0, "probs", [P, PBUF, N])
            msk = sbuf(l0, "mask", [P, RB, N], BF16)
            prologue(nc, a, sem, sbuf, (sc, trp, cx, ms), ident, mhalf, kst, v, q_dram, s_id, s_mh)
            layer0(nc, a, sem, sbuf, (sc, trp, cx, ms), ident, mhalf, whx, kst, v, pb, msk,
                   q_dram, x1_dram, s_id)
        layer1(nc, a, sem, sbuf, (sc, trp, cx, ms), ident, mhalf, whx, x1_dram, out)


def prologue(nc, a, sem, sbuf, psum, ident, mhalf, kst, v, q_dram, s_id, s_mh):
    sc, trp, cx, ms = psum
    NW = N // W
    banks = [sc[:, 0, 0:W], sc[:, 0, W:2 * W], sc[:, 1, 0:W], sc[:, 1, W:2 * W],
             trp[:, 0, :], trp[:, 1, :]]
    NBK = len(banks)
    with ExitStack() as ctx:
        xT = sbuf(ctx, "xT", [P, C, N])
        wk = sbuf(ctx, "wk", [P, C, D])
        wq = sbuf(ctx, "wq", [P, C, D])
        wv = sbuf(ctx, "wv", [P, C, D])
        bk = sbuf(ctx, "bk", [P, C])
        bq = sbuf(ctx, "bq", [P, C])
        bv = sbuf(ctx, "bv", [P, D])
        khi = sbuf(ctx, "k_hi", [P, G, N], F16)
        klo = sbuf(ctx, "k_lo", [P, G, N], F16)
        qhi = sbuf(ctx, "q_hi", [P, G, N], F16)
        qlo = sbuf(ctx, "q_lo", [P, G, N], F16)
        s_x = [sem(f"s_x{n}") for n in range(NW)]
        s_wk, s_wq, s_wv = sem("s_wk"), sem("s_wq"), sem("s_wv")
        s_pr, s_hi, s_lo, s_vd = sem("s_proj"), sem("s_hi"), sem("s_lo"), sem("s_vdone")
        s_kst, s_qdr = sem("s_kstack"), sem("s_qdram")

        jobs = [("k", g, n) for g in range(G) for n in range(NW)]
        jobs += [("q", g, n) for g in range(G) for n in range(NW)]
        jobs += [("v", r, 0) for r in range(KC // 2)]
        NKQ = 2 * G * NW
        block = ctx.enter_context(nc.Block())

        @block.sync
        def _(sp):
            sp.dma_start(wk[:, :, :], a["L0_gnn_WkT"].rearrange("(c p) m -> p c m", p=P)).then_inc(s_wk, 16)
            sp.dma_start(bk[:, :], a["L0_gnn_bk_cols"]).then_inc(s_wk, 16)
            for n in range(NW):
                sp.dma_start(xT[:, :, n * W:(n + 1) * W],
                             a["xT"].rearrange("(c p) n -> p c n", p=P)[:, :, n * W:(n + 1) * W]).then_inc(s_x[n], 16)
            sp.dma_start(wq[:, :, :], a["L0_gnn_WqT"].rearrange("(c p) m -> p c m", p=P)).then_inc(s_wq, 16)
            sp.dma_start(bq[:, :], a["L0_gnn_bq_cols"]).then_inc(s_wq, 16)
            sp.dma_start(wv[:, :, :], a["L0_gnn_WvT"].rearrange("(c p) m -> p c m", p=P)).then_inc(s_wv, 16)
            sp.dma_start(bv[:, :], a["L0_gnn_bv"].partition_broadcast(P)).then_inc(s_wv, 16)
            for g in range(G):
                sp.wait_ge(s_hi, NW * (g + 1))
                sp.wait_ge(s_lo, NW * (g + 1))
                for hh in range(HG):
                    for r in range(4):
                        src = khi if r % 2 == 0 else klo
                        sp.dma_start(kst[32 * r:32 * r + 32, g * HG + hh, :],
                                     src[DK * hh:DK * hh + DK, g, :]).then_inc(s_kst, 16)
            sp.wait_ge(s_hi, NKQ)
            sp.wait_ge(s_lo, NKQ)
            for part, src in enumerate((qhi, qlo)):
                sp.dma_start(q_dram[part].rearrange("(g p) n -> p g n", p=P), src[:, :, :]).then_inc(s_qdr, 16)
            sp.wait_ge(s_kst, 16 * G * HG * 4)
            sp.wait_ge(s_qdr, 32)

        @block.gpsimd
        def _(pool):
            nc.gpsimd.memset(ident[:, :], 0.0).then_inc(s_id, 1)
            nc.gpsimd.memset(mhalf[:, :], -0.5).then_inc(s_mh, 1)
            pool.wait_ge(s_id, 1)
            nc.gpsimd.affine_select(out=ident[:, :], in_=ident[:, :], compare_op=ALU.not_equal, fill=1.0,
                                    base=0, pattern=[[-1, P]], channel_multiplier=1).then_inc(s_id, 1)

        @block.tensor
        def _(pe):
            pe.wait_ge(s_wk, 32)
            for i, (what, g, n) in enumerate(jobs):
                bank = banks[i % NBK]
                if (what, g, n) == ("q", 0, 0):
                    pe.wait_ge(s_wq, 32)
                if (what, g, n) == ("v", 0, 0):
                    pe.wait_ge(s_wv, 32)
                if what == "k" and g == 0:
                    pe.wait_ge(s_x[n], 16)
                back = i - NBK
                if back >= 0:
                    if back < NKQ:
                        pe.wait_ge(s_lo, back + 1)
                    else:
                        pe.wait_ge(s_vd, back - NKQ + 1)
                if what in "kq":
                    w = wk if what == "k" else wq
                    for c in range(C):
                        mm = nc.tensor.matmul(bank, w[:, c, g * P:(g + 1) * P], xT[:, c, n * W:(n + 1) * W],
                                              start=(c == 0), stop=(c == C - 1))
                else:
                    for j in range(2):
                        r = 2 * g + j
                        for c in range(C):
                            mm = nc.tensor.matmul(bank[:, j * D:(j + 1) * D], xT[:, c, r * P:(r + 1) * P],
                                                  wv[:, c, :], start=(c == 0), stop=(c == C - 1))
                mm.then_inc(s_pr, 1)

        @block.scalar
        def _(act):
            for i, (what, g, n) in enumerate(jobs[:NKQ]):
                hi, b = (khi, bk) if what == "k" else (qhi, bq)
                act.wait_ge(s_pr, i + 1)
                if i == G * NW:
                    act.wait_ge(s_wq, 32)
                nc.scalar.activation(hi[:, g, n * W:(n + 1) * W], banks[i % NBK], ACT.Identity,
                                     bias=b[:, g:g + 1]).then_inc(s_hi, 1)

        @block.vector
        def _(dve):
            for i, (what, g, n) in enumerate(jobs):
                bank = banks[i % NBK]
                dve.wait_ge(s_pr, i + 1)
                if what == "v":
                    if g == 0:
                        dve.wait_ge(s_wv, 32)
                    for j in range(2):
                        add = nc.vector.tensor_tensor(v[:, 2 * g + j, :], bank[:, j * D:(j + 1) * D], bv[:, :], ALU.add)
                    add.then_inc(s_vd, 1)
                    continue
                hi, lo, b = (khi, klo, bk) if what == "k" else (qhi, qlo, bq)
                dve.wait_ge(s_hi, i + 1)
                nc.vector.scalar_tensor_tensor(out=lo[:, g, n * W:(n + 1) * W], in0=bank, scalar=b[:, g:g + 1],
                                               in1=hi[:, g, n * W:(n + 1) * W], op0=ALU.add,
                                               op1=ALU.subtract).then_inc(s_lo, 1)


def layer0(nc, a, sem, sbuf, psum, ident, mhalf, whx, kst, v, pb, msk, q_dram, x1_dram, s_id):
    sc, trp, cx, ms = psum
    MC = FF // P
    TAIL_USES = 13
    with ExitStack() as ctx:
        qst = sbuf(ctx, "q_stack", [P, H, QB], F16)
        pt = sbuf(ctx, "probs_T", [P, HG, KC, QB])
        adj_half = sbuf(ctx, "adj_half", [P, HALF], I32)
        adj_diag = sbuf(ctx, "adj_diag", [P, P], I32)
        ident_i = sbuf(ctx, "ident_i", [P, P], I32)
        wo = sbuf(ctx, "wo", [P, C, D])
        w1 = sbuf(ctx, "w1", [P, C, FF])
        w2 = sbuf(ctx, "w2", [P, MC, D])
        b1 = sbuf(ctx, "b1", [P, MC])
        rows = {n: sbuf(ctx, n, [P, D]) for n in
                ("bo", "b2", "ln1_g", "ln1_b", "ln2_g", "ln2_b", "n1_g", "n1_b")}
        wl = sbuf(ctx, "w_l1", [P, C, DK])
        sel = sbuf(ctx, "wh_select", [DK, DK + 2])
        xr = sbuf(ctx, "x_rows", [P, RB, D])
        ctxT = sbuf(ctx, "ctx_T", [P, G, QB])
        rdT = sbuf(ctx, "rden_T", [P, QB])
        rdw = sbuf(ctx, "rden_wide", [P, RB, HG, DK])
        h1 = sbuf(ctx, "h1", [P, RB, D])
        xr2 = sbuf(ctx, "ffn_rows", [P, RB, D])
        diag_m = sbuf(ctx, "diag_mask", [P, P], BF16)
        hT = sbuf(ctx, "h_T", [P, C, QB])
        reluT = sbuf(ctx, "relu_T", [P, MC // 2, QB])
        whT = sbuf(ctx, "wh_T", [DK, QB])
        nmax = sbuf(ctx, "neg_max", [P, PBUF, 2])
        rs = sbuf(ctx, "row_sum", [P, TPB])
        rd = sbuf(ctx, "rden", [P, RB * HG])
        st = sbuf(ctx, "ln_stats", [P, RB, 6])
        mv = sbuf(ctx, "ln_mv", [P, RB, 2])
        ve = sbuf(ctx, "ln_rstd", [P, RB])

        s_w = sem("s_weights")
        NWT = 16
        s_ii = sem("s_ident_i")
        s_q = [sem(f"s_q{g}") for g in range(G)]
        s_adj, s_dg = sem("s_adj_half"), sem("s_adj_diag")
        s_cvh, s_cvm, s_mask = sem("s_half_converted"), sem("s_diag_mask"), sem("s_mask")
        s_qk, s_ttr, s_exp, s_tr = sem("s_qk"), sem("s_max"), sem("s_exp"), sem("s_transposed")
        s_eva, s_evd = sem("s_evac_act"), sem("s_evac_dve")
        s_rd, s_rdw = sem("s_rden"), sem("s_rden_wide")
        s_pv, s_ctx = sem("s_pv"), sem("s_ctx")
        s_ms, s_mse = sem("s_misc_written"), sem("s_misc_read")
        s_xr, s_xb = sem("s_x_rows"), sem("s_x_plus_bo")
        s_bn, s_ag, s_ve, s_rstd = sem("s_bn"), sem("s_aggr"), sem("s_var_eps"), sem("s_rstd")
        s_nrm, s_g, s_gb = sem("s_norm"), sem("s_gain"), sem("s_layernorm")
        s_h1b, s_x1o = sem("s_h1_plus_b2"), sem("s_x1_stored")

        def misc_base(sb):
            return 2 + TAIL_USES * (sb - 1) if not (isinstance(sb, int) and sb == 0) else 0

        def rden_use(sb, g, tail):
            return misc_base(sb) + ((6, TAIL_USES - 1)[g] if tail else g)

        block = ctx.enter_context(nc.Block())

        def looped(eng, body, tail):
            body(0, False, False)
            eng.wait_ge(s_w, 16 * NWT)
            with eng.Fori(1, NB - 1) as sb:
                body(sb, True, False)
            body(NB - 1, True, True)
            tail(NB)

        @block.sync
        def _(sp):
            hold = holder(sp, sem("s_hold_sp"))

            def load_q(sb, g):
                for r in range(4):
                    src = q_dram[r // 2, g * P:(g + 1) * P, bass.ds(sb * QB, QB)]
                    sp.dma_start(qst[32 * r:32 * r + 32, g * HG:(g + 1) * HG, :],
                                 src.rearrange("(h d) n -> d h n", d=DK)).then_inc(s_q[g], 16)

            def load_adj(sb, b, half):
                k = (sb * RB + b) * 2 + half
                wait(sp, s_cvh, k)
                hold()
                sp.dma_start(adj_half[:, :], a["adj"][bass.ds(sb * QB + b * P, P),
                                                      half * HALF:(half + 1) * HALF]).then_inc(s_adj, 16)

            def load_diag(sb, b):
                wait(sp, s_cvm, 2 * (sb * RB + b))
                hold()
                sp.dma_start(adj_diag[:, :], a["adj"][bass.ds(sb * QB + b * P, P),
                                                      bass.ds(sb * QB + b * P, P)]).then_inc(s_dg, 16)

            def load_x(sb):
                sp.dma_start(xr[:, :, :], a["x"][bass.ds(sb * QB, QB), :].rearrange("(b p) d -> p b d", p=P))\
                    .then_inc(s_xr, 16)

            def store_x1(of):
                sp.wait_ge(s_gb, 3 * of + 2)
                hold()
                sp.dma_start(x1_dram[bass.ds(of * QB, QB), :].rearrange("(b p) d -> p b d", p=P), h1[:, :, :])\
                    .then_inc(s_x1o, 16)

            sp.dma_start(ident_i[:, :], a["ident_i"]).then_inc(s_ii, 16)
            load_diag(0, 0)
            load_adj(0, 0, 0)
            load_q(0, 0)
            load_adj(0, 0, 1)
            load_q(0, 1)
            load_diag(0, 1)
            load_adj(0, 1, 0)
            load_adj(0, 1, 1)
            sp.dma_start(wo[:, :, :], a["L0_gnn_WoT"].rearrange("(c p) m -> p c m", p=P)).then_inc(s_w, 16)
            sp.dma_start(w1[:, :, :], a["L0_gnn_W1T"].rearrange("(c p) m -> p c m", p=P)).then_inc(s_w, 16)
            sp.dma_start(w2[:, :, :], a["L0_gnn_W2T"].rearrange("(c p) m -> p c m", p=P)).then_inc(s_w, 16)
            sp.dma_start(b1[:, :], a["L0_gnn_b1_cols"]).then_inc(s_w, 16)
            for n, src in (("bo", "L0_gnn_bo"), ("b2", "L0_gnn_b2"), ("ln1_g", "L0_gnn_ln1_g"),
                           ("ln1_b", "L0_gnn_ln1_b"), ("ln2_g", "L0_gnn_ln2_g"), ("ln2_b", "L0_gnn_ln2_b"),
                           ("n1_g", "L1_gnn_ln1_g"), ("n1_b", "L1_gnn_ln1_b")):
                sp.dma_start(rows[n][:, :], a[src].partition_broadcast(P)).then_inc(s_w, 16)
            sp.dma_start(wl[:, :, :], a["L1_gnn_W"].rearrange("(c p) m -> p c m", p=P)).then_inc(s_w, 16)
            sp.dma_start(sel[:, 0:DK], a["ident"][0:DK, 0:DK]).then_inc(s_w, 16)
            for j in range(2):
                sp.dma_start(sel[:, DK + j:DK + j + 1], a["L1_gnn_a"][j * DK:(j + 1) * DK, :]).then_inc(s_w, 16)

            def body(sb, tail, last):
                if tail:
                    sp.wait_ge(s_mse, misc_base(sb) + 1)
                    hold()
                load_x(sb)
                if not last:
                    load_diag(sb + 1, 0)
                    load_adj(sb + 1, 0, 0)
                    sp.wait_ge(s_qk, 2 * (TPB * sb + TPB // 2))
                    hold()
                    load_q(sb + 1, 0)
                    load_adj(sb + 1, 0, 1)
                if tail:
                    store_x1(sb - 1)
                if not last:
                    sp.wait_ge(s_qk, 2 * (TPB * sb + TPB))
                    hold()
                    load_q(sb + 1, 1)
                    load_diag(sb + 1, 1)
                    load_adj(sb + 1, 1, 0)
                    load_adj(sb + 1, 1, 1)

            looped(sp, body, lambda sb: store_x1(sb - 1))
            sp.wait_ge(s_x1o, 16 * NB)

        @block.gpsimd
        def _(pool):
            hold = holder(pool, sem("s_hold_pool"))

            def convert(sb, b, ahead):
                k = sb * RB + b
                if ahead:
                    wait(pool, s_ttr, 2 * (TPB * (sb - 1) + TPB // 2 + (b + 1) * HG))
                for half in range(2):
                    wait(pool, s_adj, 16 * (2 * k + half + 1))
                    hold()
                    nc.gpsimd.tensor_scalar(msk[:, b, half * HALF:(half + 1) * HALF], adj_half[:, :], 0, NEG,
                                            ALU.is_equal, ALU.mult).then_inc(s_cvh, 1)
                wait(pool, s_dg, 16 * (k + 1))
                nc.gpsimd.tensor_tensor(adj_diag[:, :], adj_diag[:, :], ident_i[:, :], ALU.add).then_inc(s_cvm, 1)
                wait(pool, s_cvm, 2 * k + 1)
                wait(pool, s_mask, k)
                hold()
                nc.gpsimd.tensor_scalar(diag_m[:, :], adj_diag[:, :], 0, NEG, ALU.is_equal, ALU.mult)\
                    .then_inc(s_cvm, 1)
                wait(pool, s_cvm, 2 * k + 2)
                wait(pool, s_cvh, 2 * k + 2)
                nc.gpsimd.tensor_copy(msk[:, b, bass.ds(sb * QB + b * P, P)], diag_m[:, :]).then_inc(s_mask, 1)

            def rstd(n):
                wait(pool, s_ag, RB * (n + 1))
                hold()
                nc.gpsimd.tensor_scalar(ve[:, :], mv[:, :, 1], EPS, None, ALU.add).then_inc(s_ve, 1)
                wait(pool, s_ve, n + 1)
                nc.gpsimd.tensor_tensor(ve[:, :], ve[:, :], mhalf[:, 0:RB], ALU.pow).then_inc(s_rstd, 1)

            def gain(n, buf, g, b):
                wait(pool, s_nrm, RB * (n + 1))
                for i in range(RB):
                    nc.gpsimd.tensor_tensor(buf[:, i, :], buf[:, i, :], rows[g][:, :], ALU.mult).then_inc(s_g, 1)
                wait(pool, s_g, RB * (n + 1))
                for i in range(RB):
                    add = nc.gpsimd.tensor_tensor(buf[:, i, :], buf[:, i, :], rows[b][:, :], ALU.add)
                add.then_inc(s_gb, 1)

            def tail_early(of):
                rstd(3 * of)
                gain(3 * of, h1, "ln1_g", "ln1_b")
                wait(pool, s_gb, 3 * of + 1)
                for i in range(RB):
                    add = nc.gpsimd.tensor_tensor(xr2[:, i, :], h1[:, i, :], rows["b2"][:, :], ALU.add)
                add.then_inc(s_h1b, 1)

            def tail_late(of):
                rstd(3 * of + 1)
                gain(3 * of + 1, h1, "ln2_g", "ln2_b")
                rstd(3 * of + 2)
                gain(3 * of + 2, xr2, "n1_g", "n1_b")

            def add_bo(sb):
                wait(pool, s_xr, 16 * (sb + 1))
                for i in range(RB):
                    add = nc.gpsimd.tensor_tensor(xr[:, i, :], xr[:, i, :], rows["bo"][:, :], ALU.add)
                add.then_inc(s_xb, 1)

            pool.wait_ge(s_ii, 16)
            convert(0, 0, False)
            convert(0, 1, False)
            pool.wait_ge(s_w, 16 * NWT)

            def body(sb, tail, last):
                if tail:
                    tail_early(sb - 1)
                add_bo(sb)
                if not last:
                    convert(sb + 1, 0, True)
                if tail:
                    tail_late(sb - 1)
                if not last:
                    convert(sb + 1, 1, True)

            def tail_alone(sb):
                tail_early(sb - 1)
                tail_late(sb - 1)

            looped(pool, body, tail_alone)

        @block.tensor
        def _(pe):
            def scores(tile, t, sb):
                g, b, hh = tile_of(t)
                if t % (RB * HG) == 0:
                    wait(pe, s_q[g], 64 * (sb + 1))
                for half in range(2):
                    wait(pe, s_ttr, 2 * (tile - 1) + half + 1)
                    for j in range(HALF // W):
                        mm = nc.tensor.matmul(sc[:, half, j * W:(j + 1) * W],
                                              qst[:, g * HG + hh, b * P:(b + 1) * P],
                                              kst[:, g * HG + hh, half * HALF + j * W:half * HALF + (j + 1) * W],
                                              start=True, stop=True)
                    mm.then_inc(s_qk, 1)

            def transposes(tile, t):
                wait(pe, s_exp, tile + 1)
                for j in range(4):
                    if j == 0:
                        wait(pe, s_evd, tile)
                    else:
                        wait(pe, s_eva, 3 * tile + j - 1)
                    for i in range(4):
                        k = 4 * j + i
                        mm = nc.tensor.transpose(trp[:, j % 2, i * P:(i + 1) * P],
                                                 pb[:, t % PBUF, k * P:(k + 1) * P], ident[:, :])
                    mm.then_inc(s_tr, 1)

            def turn_rden(u, n):
                wait(pe, s_mse, u)
                wait(pe, s_rdw, n + 1)
                for b in range(RB):
                    mm = nc.tensor.transpose(ms[:, b * P:(b + 1) * P],
                                             rdw[:, b, :, :].rearrange("p h d -> p (h d)"), ident[:, :])
                mm.then_inc(s_ms, 1)

            def pv(tile, g, n):
                wait(pe, s_eva, 3 * (tile + 1))
                wait(pe, s_evd, tile + 1)
                wait(pe, s_ctx, n)
                for k in range(KC):
                    for hh in range(HG):
                        mm = nc.tensor.matmul(cx[DK * hh:DK * hh + DK, 0:QB],
                                              v[:, k, g * P + DK * hh:g * P + DK * hh + DK],
                                              pt[:, hh, k, :], start=(k == 0), stop=(k == KC - 1))
                mm.then_inc(s_pv, 1)

            def attention_out(u, of):
                wait(pe, s_mse, u)
                wait(pe, s_ctx, G * (of + 1))
                for b in range(RB):
                    for g in range(G):
                        mm = nc.tensor.matmul(ms[:, b * D:(b + 1) * D], ctxT[:, g, b * P:(b + 1) * P],
                                              wo[:, g, :], start=(g == 0), stop=(g == G - 1))
                mm.then_inc(s_ms, 1)

            def turn_rows(u, n, buf):
                wait(pe, s_mse, u)
                wait(pe, s_gb, n)
                for c in range(C):
                    for b in range(RB):
                        mm = nc.tensor.transpose(ms[:, c * QB + b * P:c * QB + (b + 1) * P],
                                                 buf[:, b, c * P:(c + 1) * P], ident[:, :])
                mm.then_inc(s_ms, 1)

            def ffn_up(u, m0):
                wait(pe, s_mse, u)
                for m in (m0, m0 + 1):
                    for c in range(C):
                        mm = nc.tensor.matmul(ms[:, (m - m0) * QB:(m - m0 + 1) * QB], w1[:, c, m * P:(m + 1) * P],
                                              hT[:, c, :], start=(c == 0), stop=(c == C - 1))
                mm.then_inc(s_ms, 1)

            def ffn_down(u, part):
                wait(pe, s_mse, u)
                for b in range(RB):
                    for m in range(MC // 2):
                        mm = nc.tensor.matmul(ms[:, b * D:(b + 1) * D], reluT[:, m, b * P:(b + 1) * P],
                                              w2[:, part * MC // 2 + m, :], start=(m == 0), stop=(m == MC // 2 - 1))
                mm.then_inc(s_ms, 1)

            def project_l1(u):
                wait(pe, s_mse, u)
                for c in range(C):
                    mm = nc.tensor.matmul(ms[0:DK, 0:QB], wl[:, c, :], hT[:, c, :], start=(c == 0), stop=(c == C - 1))
                mm.then_inc(s_ms, 1)

            def split_l1(u):
                wait(pe, s_mse, u)
                for b in range(RB):
                    mm = nc.tensor.matmul(ms[:, b * (DK + 2):(b + 1) * (DK + 2)], whT[:, b * P:(b + 1) * P],
                                          sel[:, :], start=True, stop=True)
                mm.then_inc(s_ms, 1)

            def tail_step(t, of, base, rden):
                if t == 1:
                    attention_out(base + 0, of)
                elif t == 3:
                    turn_rows(base + 1, 3 * of + 1, h1)
                elif t == 4:
                    ffn_up(base + 2, 0)
                elif t == 5:
                    ffn_up(base + 3, 2)
                elif t == 6:
                    ffn_down(base + 4, 0)
                elif t == 7:
                    ffn_up(base + 5, 4)
                elif t == 8:
                    ffn_up(base + rden + 6, 6)
                elif t == 9:
                    ffn_down(base + rden + 7, 1)
                elif t == 13:
                    turn_rows(base + rden + 8, 3 * of + 3, xr2)
                elif t == 14:
                    project_l1(base + rden + 9)
                elif t == 15:
                    split_l1(base + rden + 10)

            pe.wait_ge(s_id, 2)
            scores(0, 0, 0)
            scores(1, 1, 0)

            def body(sb, tail, last):
                for t in range(TPB):
                    tile = TPB * sb + t
                    turns = t % (TPB // G) == TPB // G - 1
                    if tail and turns:
                        tail_step(t, sb - 1, misc_base(sb), 1)
                    if not (last and t + 2 >= TPB):
                        scores(tile + 2, (t + 2) % TPB, sb + (t + 2) // TPB)
                    transposes(tile, t)
                    if tail and not turns:
                        tail_step(t, sb - 1, misc_base(sb), 1)
                    if turns:
                        g = tile_of(t)[0]
                        turn_rden(rden_use(sb, g, tail), G * sb + g)
                        pv(tile, g, G * sb + g)

            def tail_alone(sb):
                for t in range(TPB):
                    tail_step(t, sb - 1, misc_base(sb), 0)

            looped(pe, body, tail_alone)

        @block.vector
        def _(dve):
            hold = holder(dve, sem("s_hold_dve"))

            def reduce_half(tile, t, half, sb):
                g, b, hh = tile_of(t)
                slot = t % PBUF
                wait(dve, s_qk, 2 * tile + half + 1)
                if half == 0:
                    wait(dve, s_tr, 4 * (tile - PBUF + 1))
                    if g == 0 and hh == 0:
                        wait(dve, s_mask, RB * sb + b + 1)
                else:
                    wait(dve, s_ttr, 2 * tile + 1)
                hold()
                nc.vector.tensor_tensor_reduce(
                    out=pb[:, slot, half * HALF:(half + 1) * HALF], in0=sc[:, half, :],
                    in1=msk[:, b, half * HALF:(half + 1) * HALF], scale=-SCALE,
                    scalar=BIG if half == 0 else nmax[:, slot, 0:1], op0=ALU.add, op1=ALU.min,
                    accum_out=nmax[:, slot, half:half + 1]).then_inc(s_ttr, 1)

            def evacuate(tile, t):
                g, b, hh = tile_of(t)
                wait(dve, s_tr, 4 * tile + 3)
                nc.vector.tensor_copy(pt[:, hh, 8:12, b * P:(b + 1) * P],
                                      trp[:, 0, :].rearrange("p (k q) -> p k q", k=4)).then_inc(s_evd, 1)

            def widen_rden(tile, g, n):
                wait(dve, s_exp, tile + 1)
                nc.vector.reciprocal(rd[:, :], rs[:, g * RB * HG:(g + 1) * RB * HG]).then_inc(s_rd, 1)
                wait(dve, s_rd, n + 1)
                for b in range(RB):
                    cp = nc.vector.tensor_copy(
                        rdw[:, b, :, :], rd[:, b * HG:(b + 1) * HG].unsqueeze(2).to_broadcast([P, HG, DK]))
                cp.then_inc(s_rdw, 1)

            def scale_ctx(g, n, u):
                wait(dve, s_pv, n + 1)
                wait(dve, s_mse, u + 1)
                nc.vector.tensor_tensor(ctxT[:, g, :], cx[:, 0:QB], rdT[:, :], ALU.mult).then_inc(s_ctx, 1)

            def statistics(n, buf):
                for i in range(RB):
                    nc.vector.bn_stats(st[:, i, :], buf[:, i, :]).then_inc(s_bn, 1)
                wait(dve, s_bn, RB * (n + 1))
                hold()
                for i in range(RB):
                    nc.vector.bn_aggr(mv[:, i, :], st[:, i, :]).then_inc(s_ag, 1)

            def normalize(n, dst, buf):
                wait(dve, s_rstd, n + 1)
                for i in range(RB):
                    nc.vector.tensor_scalar(dst[:, i, :], buf[:, i, :], mv[:, i, 0:1], ve[:, i:i + 1],
                                            ALU.subtract, ALU.mult).then_inc(s_nrm, 1)

            msv = ms[:, :].rearrange("p (b d) -> p b d", b=RB)

            def tail_step(t, of, base, rden):
                if t == 1:
                    wait(dve, s_ms, base + 1)
                    wait(dve, s_xb, of + 1)
                    wait(dve, s_x1o, 16 * of)
                    nc.vector.tensor_tensor(h1[:, :, :], msv, xr[:, :, :], ALU.add).then_inc(s_mse, 1)
                    wait(dve, s_mse, base + 1)
                    statistics(3 * of, h1)
                elif t == 2:
                    normalize(3 * of, h1, h1)
                elif t == 6:
                    wait(dve, s_ms, base + 5)
                    wait(dve, s_h1b, of + 1)
                    nc.vector.tensor_tensor(xr2[:, :, :], msv, xr2[:, :, :], ALU.add).then_inc(s_mse, 1)
                elif t == 9:
                    u = base + rden + 7
                    wait(dve, s_ms, u + 1)
                    nc.vector.tensor_tensor(xr2[:, :, :], msv, xr2[:, :, :], ALU.add).then_inc(s_mse, 1)
                    wait(dve, s_mse, u + 1)
                    statistics(3 * of + 1, xr2)
                elif t == 10:
                    normalize(3 * of + 1, h1, xr2)
                elif t == 11:
                    wait(dve, s_gb, 3 * of + 2)
                    statistics(3 * of + 2, h1)
                elif t == 12:
                    normalize(3 * of + 2, xr2, h1)
                elif t == 14:
                    u = base + rden + 9
                    wait(dve, s_ms, u + 1)
                    nc.vector.tensor_copy(whT[:, :], ms[0:DK, 0:QB]).then_inc(s_mse, 1)
                elif t == 15:
                    u = base + rden + 10
                    wait(dve, s_ms, u + 1)
                    nc.vector.tensor_copy(whx[:, bass.ds(of * RB, RB), :],
                                          ms[:, 0:RB * (DK + 2)].rearrange("p (b d) -> p b d", b=RB))\
                        .then_inc(s_mse, 1)

            reduce_half(0, 0, 0, 0)
            reduce_half(0, 0, 1, 0)
            reduce_half(1, 1, 0, 0)
            reduce_half(1, 1, 1, 0)

            def body(sb, tail, last):
                for t in range(TPB):
                    tile = TPB * sb + t
                    turns = t % (TPB // G) == TPB // G - 1
                    if tail and turns:
                        tail_step(t, sb - 1, misc_base(sb), 1)
                    if turns:
                        widen_rden(tile, tile_of(t)[0], G * sb + tile_of(t)[0])
                    ahead = not (last and t + 2 >= TPB)
                    if ahead:
                        reduce_half(tile + 2, (t + 2) % TPB, 0, sb + (t + 2) // TPB)
                    if t == TPB // G:
                        scale_ctx(0, G * sb, rden_use(sb, 0, tail))
                    if t == 0 and tail:
                        scale_ctx(1, G * sb - 1, misc_base(sb) - 1)
                    evacuate(tile, t)
                    if ahead:
                        reduce_half(tile + 2, (t + 2) % TPB, 1, sb + (t + 2) // TPB)
                    if tail and not turns:
                        tail_step(t, sb - 1, misc_base(sb), 1)

            def tail_alone(sb):
                scale_ctx(1, G * sb - 1, misc_base(sb) - 1)
                for t in range(TPB):
                    tail_step(t, sb - 1, misc_base(sb), 0)

            looped(dve, body, tail_alone)

        @block.scalar
        def _(act):
            def exponentiate(tile, t):
                slot = t % PBUF
                wait(act, s_ttr, 2 * tile + 2)
                nc.scalar.activation(pb[:, slot, :], pb[:, slot, :], ACT.Exp, bias=nmax[:, slot, 1:2], scale=-1.0,
                                     accum_out=rs[:, t:t + 1]).then_inc(s_exp, 1)

            def evacuate(tile, t, j):
                g, b, hh = tile_of(t)
                wait(act, s_tr, 4 * tile + j + 1)
                nc.scalar.activation(pt[:, hh, 4 * j:4 * j + 4, b * P:(b + 1) * P],
                                     trp[:, j % 2, :].rearrange("p (k q) -> p k q", k=4), ACT.Copy)\
                    .then_inc(s_eva, 1)

            def copy_rden(u, n):
                wait(act, s_ms, u + 1)
                wait(act, s_ctx, n)
                nc.scalar.activation(rdT[:, :], ms[:, 0:QB], ACT.Copy).then_inc(s_mse, 1)

            def tail_step(t, of, base, rden):
                if t in (3, 13):
                    u = base + (1 if t == 3 else rden + 8)
                    wait(act, s_ms, u + 1)
                    nc.scalar.activation(hT[:, :, :], ms[:, :].rearrange("p (c q) -> p c q", c=C), ACT.Copy)\
                        .then_inc(s_mse, 1)
                elif t in (4, 5, 7, 8):
                    m0 = {4: 0, 5: 2, 7: 4, 8: 6}[t]
                    u = base + {4: 2, 5: 3, 7: 5, 8: rden + 6}[t]
                    wait(act, s_ms, u + 1)
                    for i in range(2):
                        relu = nc.scalar.activation(reluT[:, (m0 + i) % (MC // 2), :], ms[:, i * QB:(i + 1) * QB],
                                                    ACT.Relu, bias=b1[:, m0 + i:m0 + i + 1])
                    relu.then_inc(s_mse, 1)

            exponentiate(0, 0)
            exponentiate(1, 1)

            def body(sb, tail, last):
                for t in range(TPB):
                    tile = TPB * sb + t
                    turns = t % (TPB // G) == TPB // G - 1
                    if tail and turns:
                        tail_step(t, sb - 1, misc_base(sb), 1)
                    for j in (0, 1, 3):
                        evacuate(tile, t, j)
                    if tail and not turns:
                        tail_step(t, sb - 1, misc_base(sb), 1)
                    if turns:
                        g = tile_of(t)[0]
                        copy_rden(rden_use(sb, g, tail), G * sb + g)
                    if not (last and t + 2 >= TPB):
                        exponentiate(tile + 2, (t + 2) % TPB)

            def tail_alone(sb):
                for t in range(TPB):
                    tail_step(t, sb - 1, misc_base(sb), 0)

            looped(act, body, tail_alone)


def layer1(nc, a, sem, sbuf, psum, ident, mhalf, whx, x1_dram, out):
    sc, trp, cx, ms = psum
    MC = HID // P
    banks = [sc[:, 0, 0:W], sc[:, 0, W:2 * W], sc[:, 1, 0:W], sc[:, 1, W:2 * W]]
    with ExitStack() as ctx:
        fdb = sbuf(ctx, "f_dst_rows", [P, N])
        x1 = sbuf(ctx, "x1_rows", [P, KC, D])
        pb = sbuf(ctx, "probs_l1", [P, 3, N])
        low = sbuf(ctx, "leaky_low", [P, 2, N])
        msk = sbuf(ctx, "mask_l1", [P, 2, N], BF16)
        adj = sbuf(ctx, "adj_l1", [P, 2, N], I32)
        pt = sbuf(ctx, "probs_T_l1", [P, 2, KC, SQ])
        fc = sbuf(ctx, "fc4", [P, D])
        fc1 = sbuf(ctx, "fc1", [P, C, HID])
        fc2 = sbuf(ctx, "fc2", [P, MC, D])
        fb1 = sbuf(ctx, "fc1_b", [P, MC])
        rows = {n: sbuf(ctx, "l1_" + n, [P, D]) for n in ("fc_b", "g", "b", "fc2_b")}
        hp = sbuf(ctx, "h_prime_T", [P, SQ])
        h2 = sbuf(ctx, "h2", [P, ST, D])
        h2T = sbuf(ctx, "h2_T", [P, C, N])
        geluT = sbuf(ctx, "gelu_T", [P, MC, SQ])
        yo = sbuf(ctx, "out_rows", [P, ST, D])
        nmax = sbuf(ctx, "neg_max_l1", [P, KC])
        rs = sbuf(ctx, "row_sum_l1", [P, KC])
        rd = sbuf(ctx, "rden_l1", [P, KC])
        st = sbuf(ctx, "stats_l1", [P, ST, 6])
        mv = sbuf(ctx, "mv_l1", [P, ST, 2])
        ve = sbuf(ctx, "rstd_l1", [P, ST])

        s_w, s_x = sem("s_l1_weights"), sem("s_l1_x1")
        NWT = 11
        s_adj = [sem(f"s_l1_adj{i}") for i in range(2)]
        s_fdt, s_fdb = sem("s_l1_fd_turned"), sem("s_l1_fd")
        s_cv, s_low, s_lr, s_max, s_exp = (sem("s_l1_" + n) for n in ("mask", "low", "leaky", "max", "exp"))
        s_tr, s_eva, s_evd = (sem("s_l1_" + n) for n in ("turned", "evac_act", "evac_dve"))
        s_pv, s_hp, s_fc, s_x2, s_rd = (sem("s_l1_" + n) for n in ("pv", "h_prime", "fc", "x2", "rden"))
        s_xb, s_bn, s_ag, s_ve, s_rstd = (sem("s_l1_" + n) for n in ("x1b", "bn", "aggr", "ve", "rstd"))
        s_nrm, s_g, s_gb, s_ht, s_hte = (sem("s_l1_" + n) for n in ("norm", "gain", "ln", "h2_turned", "h2T"))
        s_up, s_ge, s_dn, s_y, s_x2b, s_out = (sem("s_l1_" + n) for n in ("up", "gelu", "down", "y", "x2b", "out"))

        block = ctx.enter_context(nc.Block())

        @block.sync
        def _(sp):
            def load_adj(t):
                wait(sp, s_cv, t - 1)
                sp.dma_start(adj[:, t % 2, :], a["adj"][t * P:(t + 1) * P, :]).then_inc(s_adj[t % 2], 16)

            load_adj(0)
            sp.dma_start(x1[:, :, :], x1_dram.rearrange("(t p) d -> p t d", p=P)).then_inc(s_x, 16)
            load_adj(1)
            for i in range(4):
                sp.dma_start(fc[DK * i:DK * i + DK, :], a["L1_gnn_fc_wT"]).then_inc(s_w, 16)
            sp.dma_start(rows["fc_b"][:, :], a["L1_gnn_fc_b"].partition_broadcast(P)).then_inc(s_w, 16)
            sp.dma_start(rows["g"][:, :], a["L1_gnn_ln2_g"].partition_broadcast(P)).then_inc(s_w, 16)
            sp.dma_start(rows["b"][:, :], a["L1_gnn_ln2_b"].partition_broadcast(P)).then_inc(s_w, 16)
            sp.dma_start(rows["fc2_b"][:, :], a["L1_gnn_fc2_b"].partition_broadcast(P)).then_inc(s_w, 16)
            sp.dma_start(fc1[:, :, :], a["L1_gnn_fc1_wT"].rearrange("(c p) m -> p c m", p=P)).then_inc(s_w, 16)
            sp.dma_start(fc2[:, :, :], a["L1_gnn_fc2_wT"].rearrange("(c p) m -> p c m", p=P)).then_inc(s_w, 16)
            sp.dma_start(fb1[:, :], a["L1_gnn_fc1_b_cols"]).then_inc(s_w, 16)
            for t in range(2, KC):
                load_adj(t)
            for s in range(NS):
                sp.wait_ge(s_y, ST * (s + 1))
                sp.dma_start(out[s * SQ:(s + 1) * SQ, :].rearrange("(t p) d -> p t d", p=P), yo[:, :, :])\
                    .then_inc(s_out, 16)
            sp.wait_ge(s_out, 16 * NS)

        @block.gpsimd
        def _(pool):
            def layernorm(s):
                wait(pool, s_ag, ST * (s + 1))
                nc.gpsimd.tensor_scalar(ve[:, :], mv[:, :, 1], EPS, None, ALU.add).then_inc(s_ve, 1)
                wait(pool, s_ve, s + 1)
                nc.gpsimd.tensor_tensor(ve[:, :], ve[:, :], mhalf[:, 0:ST], ALU.pow).then_inc(s_rstd, 1)
                wait(pool, s_nrm, ST * (s + 1))
                for i in range(ST):
                    nc.gpsimd.tensor_tensor(h2[:, i, :], h2[:, i, :], rows["g"][:, :], ALU.mult).then_inc(s_g, 1)
                wait(pool, s_g, ST * (s + 1))
                for i in range(ST):
                    add = nc.gpsimd.tensor_tensor(h2[:, i, :], h2[:, i, :], rows["b"][:, :], ALU.add)
                add.then_inc(s_gb, 1)
                for i in range(ST):
                    t = s * ST + i
                    add = nc.gpsimd.tensor_tensor(x1[:, t, :], x1[:, t, :], rows["fc2_b"][:, :], ALU.add)
                add.then_inc(s_x2b, 1)

            for t in range(KC):
                wait(pool, s_max, t - 1)
                wait(pool, s_adj[t % 2], 16 * (t // 2 + 1))
                nc.gpsimd.tensor_scalar(msk[:, t % 2, :], adj[:, t % 2, :], 0, NEG, ALU.is_le, ALU.mult)\
                    .then_inc(s_cv, 1)
                if t == 0:
                    pool.wait_ge(s_fdb, 4)
                wait(pool, s_lr, t - 1)
                nc.gpsimd.tensor_scalar(low[:, t % 2, :], fdb[:, :], whx[:, t, DK:DK + 1], 0.2, ALU.add, ALU.mult)\
                    .then_inc(s_low, 1)
                if t == 0:
                    pool.wait_ge(s_w, 16 * NWT)
                    pool.wait_ge(s_x, 16)
                if t % ST == 0:
                    for i in range(ST):
                        add = nc.gpsimd.tensor_tensor(x1[:, t + i, :], x1[:, t + i, :], rows["fc_b"][:, :], ALU.add)
                    add.then_inc(s_xb, 1)
                if t % ST == 2 and t > ST:
                    layernorm(t // ST - 1)
            layernorm(NS - 1)

        @block.tensor
        def _(pe):
            for k in range(KC):
                mm = nc.tensor.transpose(banks[k // 4][:, (k % 4) * P:(k % 4 + 1) * P],
                                         whx[:, k, DK + 1:DK + 2].to_broadcast([P, P]), ident[:, :])
                if k % 4 == 3:
                    mm.then_inc(s_fdt, 1)

            def turn_h2(s):
                wait(pe, s_gb, s + 1)
                for c in range(C):
                    bank = (ms[:, :], cx[:, :])[c]
                    if c == 1:
                        wait(pe, s_hp, min(s + 2, NS))
                    wait(pe, s_hte, C * s + c - 1)
                    for i in range(ST):
                        mm = nc.tensor.transpose(bank[:, i * P:(i + 1) * P], h2[:, i, c * P:(c + 1) * P], ident[:, :])
                    mm.then_inc(s_ht, 1)

            for t in range(KC):
                s, i = t // ST, t % ST
                wait(pe, s_exp, t + 1)
                for j in range(4):
                    if t == 0:
                        wait(pe, s_fdb, j + 1)
                    elif j % 2 == 0:
                        wait(pe, s_eva, 2 * (t - 1) + j // 2 + 1)
                    else:
                        wait(pe, s_evd, 2 * (t - 1) + j // 2 + 1)
                    for m in range(4):
                        k = 4 * j + m
                        mm = nc.tensor.transpose(banks[j][:, m * P:(m + 1) * P], pb[:, t % 3, k * P:(k + 1) * P],
                                                 ident[:, :])
                    mm.then_inc(s_tr, 1)
                if i == ST - 1:
                    wait(pe, s_eva, 2 * (t + 1))
                    wait(pe, s_evd, 2 * (t + 1))
                    wait(pe, s_hp, s)
                    wait(pe, s_hte, C * (s - 1))
                    for k in range(KC):
                        c = k % 4
                        mm = nc.tensor.matmul(cx[DK * c:DK * c + DK, :], whx[:, k, 0:DK], pt[:, s % 2, k, :],
                                              start=(k < 4), stop=(k >= KC - 4))
                    mm.then_inc(s_pv, 1)
                    pe.wait_ge(s_w, 16 * NWT)
                    wait(pe, s_hp, s + 1)
                    wait(pe, s_x2, ST * s)
                    for m in range(ST):
                        mm = nc.tensor.matmul(trp[:, m // 2, (m % 2) * D:(m % 2 + 1) * D], hp[:, m * P:(m + 1) * P],
                                              fc[:, :], start=True, stop=True)
                        mm.then_inc(s_fc, 1)
                if i == 3 and s >= 1:
                    turn_h2(s - 1)
            turn_h2(NS - 1)
            for s in range(NS):
                if s == 0:
                    wait(pe, s_eva, 2 * KC)
                    wait(pe, s_evd, 2 * KC)
                wait(pe, s_hte, C * (s + 1))
                for m in range(MC):
                    wait(pe, s_ge, MC * (s - 1) + m + 1)
                    for c in range(C):
                        mm = nc.tensor.matmul(banks[m], fc1[:, c, m * P:(m + 1) * P], h2T[:, c, s * SQ:(s + 1) * SQ],
                                              start=(c == 0), stop=(c == C - 1))
                    mm.then_inc(s_up, 1)
                wait(pe, s_x2, ST * NS)
                wait(pe, s_ge, MC * (s + 1))
                for i in range(ST):
                    wait(pe, s_y, ST * (s - 1) + 2 * (i // 2) + 2)
                    for m in range(MC):
                        mm = nc.tensor.matmul(trp[:, i // 2, (i % 2) * D:(i % 2 + 1) * D],
                                              geluT[:, m, i * P:(i + 1) * P], fc2[:, m, :],
                                              start=(m == 0), stop=(m == MC - 1))
                    mm.then_inc(s_dn, 1)

        @block.scalar
        def _(act):
            for j in range(4):
                act.wait_ge(s_fdt, j + 1)
                nc.scalar.activation(fdb[:, j * W:(j + 1) * W], banks[j], ACT.Copy).then_inc(s_fdb, 1)

            def copy_h2(s):
                for c in range(C):
                    wait(act, s_ht, C * s + c + 1)
                    nc.scalar.activation(h2T[:, c, s * SQ:(s + 1) * SQ], (ms[:, :], cx[:, :])[c], ACT.Copy)\
                        .then_inc(s_hte, 1)

            def exponentiate(t):
                wait(act, s_max, t + 1)
                nc.scalar.activation(pb[:, t % 3, :], pb[:, t % 3, :], ACT.Exp, bias=nmax[:, t:t + 1], scale=-1.0,
                                     accum_out=rs[:, t:t + 1]).then_inc(s_exp, 1)

            exponentiate(0)
            for t in range(KC):
                s, i = t // ST, t % ST
                if t + 1 < KC:
                    exponentiate(t + 1)
                for j in (0, 2):
                    wait(act, s_tr, 4 * t + j + 1)
                    nc.scalar.activation(pt[:, s % 2, 4 * j:4 * j + 4, i * P:(i + 1) * P],
                                         banks[j].rearrange("p (k q) -> p k q", k=4), ACT.Copy).then_inc(s_eva, 1)
                if i == ST - 1:
                    wait(act, s_pv, s + 1)
                    wait(act, s_fc, ST * s)
                    nc.scalar.activation(hp[:, :], cx[:, :], ACT.Copy).then_inc(s_hp, 1)
                    if s >= 1:
                        copy_h2(s - 1)
            copy_h2(NS - 1)
            act.wait_ge(s_w, 16 * NWT)
            for s in range(NS):
                wait(act, s_dn, ST * s)
                for m in range(MC):
                    wait(act, s_up, MC * s + m + 1)
                    nc.scalar.activation(geluT[:, m, :], banks[m], ACT.Gelu, bias=fb1[:, m:m + 1]).then_inc(s_ge, 1)

        @block.vector
        def _(dve):
            def leaky(t):
                wait(dve, s_low, t + 1)
                wait(dve, s_tr, 4 * (t - 2))
                nc.vector.scalar_tensor_tensor(out=pb[:, t % 3, :], in0=fdb[:, :], scalar=whx[:, t, DK:DK + 1],
                                               in1=low[:, t % 2, :], op0=ALU.add, op1=ALU.max).then_inc(s_lr, 1)
                wait(dve, s_lr, t + 1)
                wait(dve, s_cv, t + 1)
                nc.vector.tensor_tensor_reduce(out=pb[:, t % 3, :], in0=pb[:, t % 3, :], in1=msk[:, t % 2, :],
                                               scale=-1.0, scalar=BIG, op0=ALU.add, op1=ALU.min,
                                               accum_out=nmax[:, t:t + 1]).then_inc(s_max, 1)

            def residual(s):
                wait(dve, s_exp, ST * (s + 1))
                nc.vector.reciprocal(rd[:, s * ST:(s + 1) * ST], rs[:, s * ST:(s + 1) * ST]).then_inc(s_rd, 1)
                wait(dve, s_rd, s + 1)
                wait(dve, s_xb, s + 1)
                for i in range(ST):
                    t = s * ST + i
                    wait(dve, s_fc, s * ST + 2 * (i // 2) + 2)
                    nc.vector.scalar_tensor_tensor(out=x1[:, t, :], in0=trp[:, i // 2, (i % 2) * D:(i % 2 + 1) * D],
                                                   scalar=rd[:, t:t + 1], in1=x1[:, t, :], op0=ALU.mult,
                                                   op1=ALU.add).then_inc(s_x2, 1)
                wait(dve, s_x2, ST * (s + 1))
                for i in range(ST):
                    nc.vector.bn_stats(st[:, i, :], x1[:, s * ST + i, :]).then_inc(s_bn, 1)
                wait(dve, s_bn, ST * (s + 1))
                for i in range(ST):
                    nc.vector.bn_aggr(mv[:, i, :], st[:, i, :]).then_inc(s_ag, 1)

            def normalize(s):
                wait(dve, s_rstd, s + 1)
                wait(dve, s_ht, C * s)
                for i in range(ST):
                    nc.vector.tensor_scalar(h2[:, i, :], x1[:, s * ST + i, :], mv[:, i, 0:1], ve[:, i:i + 1],
                                            ALU.subtract, ALU.mult).then_inc(s_nrm, 1)

            dve.wait_ge(s_fdb, 4)
            leaky(0)
            for t in range(KC):
                s, i = t // ST, t % ST
                if t + 1 < KC:
                    leaky(t + 1)
                for j in (1, 3):
                    wait(dve, s_tr, 4 * t + j + 1)
                    nc.vector.tensor_copy(pt[:, s % 2, 4 * j:4 * j + 4, i * P:(i + 1) * P],
                                          banks[j].rearrange("p (k q) -> p k q", k=4)).then_inc(s_evd, 1)
                if i == 0 and s >= 1:
                    residual(s - 1)
                if i == 1 and s >= 1:
                    normalize(s - 1)
            residual(NS - 1)
            normalize(NS - 1)
            for s in range(NS):
                wait(dve, s_x2b, s + 1)
                wait(dve, s_out, 16 * s)
                for i in range(ST):
                    t = s * ST + i
                    wait(dve, s_dn, s * ST + 2 * (i // 2) + 2)
                    nc.vector.tensor_tensor(yo[:, i, :], trp[:, i // 2, (i % 2) * D:(i % 2 + 1) * D], x1[:, t, :],
                                            ALU.add).then_inc(s_y, 1)


TRANSPOSED = ("L0_gnn_Wq", "L0_gnn_Wk", "L0_gnn_Wv", "L0_gnn_Wo", "L0_gnn_W1", "L0_gnn_W2",
              "L1_gnn_fc_w", "L1_gnn_fc1_w", "L1_gnn_fc2_w")
COLUMNS = ("L0_gnn_bq", "L0_gnn_bk", "L0_gnn_b1", "L1_gnn_fc1_b")
AS_IS = ("x", "adj", "L0_gnn_bv", "L0_gnn_bo", "L0_gnn_b2",
         "L0_gnn_ln1_g", "L0_gnn_ln1_b", "L0_gnn_ln2_g", "L0_gnn_ln2_b", "L1_gnn_W", "L1_gnn_a",
         "L1_gnn_fc_b", "L1_gnn_ln1_g", "L1_gnn_ln1_b", "L1_gnn_ln2_g", "L1_gnn_ln2_b",
         "L1_gnn_fc2_b")


def kernel(**inputs):
    import concourse.bacc as bacc
    from concourse.bass_utils import run_bass_kernel_spmd

    host = {n: np.ascontiguousarray(inputs[n]) for n in AS_IS}
    host.update({n + "T": np.ascontiguousarray(np.asarray(inputs[n]).T) for n in ("x",) + TRANSPOSED})
    for n in COLUMNS:
        host[n + "_cols"] = np.ascontiguousarray(np.asarray(inputs[n]).reshape(-1, P).T)
    host["ident"] = np.eye(P, dtype=np.float32)
    host["ident_i"] = np.eye(P, dtype=np.int32)
    nc = bacc.Bacc("TRN2", target_bir_lowering=False, num_devices=1)
    aps = {n: nc.dram_tensor(f"in_{n}", x.shape, mybir.dt.from_np(x.dtype), kind="ExternalInput").ap()
           for n, x in host.items()}
    out = nc.dram_tensor("out_rows_dram", (N, D), F32, kind="ExternalOutput").ap()
    build(nc, aps, out)
    r = run_bass_kernel_spmd(nc, [{f"in_{n}": x for n, x in host.items()}], core_ids=[0])
    return r.results[0]["out_rows_dram"]
```

```python
from contextlib import ExitStack

import numpy as np

import concourse.bass as bass
from concourse import mybir

ALU = mybir.AluOpType
ACT = mybir.ActivationFunctionType
F32 = mybir.dt.float32
F16 = mybir.dt.float16
BF16 = mybir.dt.bfloat16
I32 = mybir.dt.int32

P = 128
N, D = 2048, 256
H = 8
DK = D // H
HG = P // DK
G = H // HG
C = D // P
FF = 1024
HID = 512
KC = N // P
QB = 256
NB = N // QB
RB = QB // P
TPB = G * RB * HG
HALF = N // 2
W = 512
PBUF = 4
NEG = -2.0 ** 100
EPS = 1e-5
SCALE = 1.0 / float(np.sqrt(np.float32(DK)))
BIG = 3.0e38
SQ = 512
NS = N // SQ
ST = SQ // P


def wait(eng, sem, value):
    if isinstance(value, int) and value <= 0:
        return
    eng.wait_ge(sem, value)


def holder(eng, sem):
    return lambda: eng.sem_inc(sem, 1)


def tile_of(t):
    return t // (RB * HG), (t % (RB * HG)) // HG, t % HG


def build(nc, a, out):
    x1_dram = nc.dram_tensor("x1_scratch", (N, D), F32, kind="Internal").ap()
    q_dram = nc.dram_tensor("q_scratch", (2, D, N), F16, kind="Internal").ap()

    with ExitStack() as whole:
        def sem(name):
            return whole.enter_context(nc.semaphore(name))

        def sbuf(ctx, name, shape, dt=F32):
            return ctx.enter_context(nc.sbuf_tensor(name, shape, dt))

        sc = whole.enter_context(nc.psum_tensor("score_ps", [P, 2, HALF], F32))
        trp = whole.enter_context(nc.psum_tensor("transpose_ps", [P, 2, W], F32))
        cx = whole.enter_context(nc.psum_tensor("context_ps", [P, W], F32))
        ms = whole.enter_context(nc.psum_tensor("misc_ps", [P, W], F32))

        ident = sbuf(whole, "ident", [P, P])
        mhalf = sbuf(whole, "minus_half", [P, 4])
        whx = sbuf(whole, "whx", [P, KC, DK + 2])

        s_id = sem("s_id")
        s_mh = sem("s_mh")

        with ExitStack() as l0:
            kst = sbuf(l0, "k_stack", [P, H, N], F16)
            v = sbuf(l0, "v", [P, KC, D])
            pb = sbuf(l0, "probs", [P, PBUF, N])
            msk = sbuf(l0, "mask", [P, RB, N], BF16)
            prologue(nc, a, sem, sbuf, (sc, trp, cx, ms), ident, mhalf, kst, v, q_dram, s_id, s_mh)
            layer0(nc, a, sem, sbuf, (sc, trp, cx, ms), ident, mhalf, whx, kst, v, pb, msk,
                   q_dram, x1_dram, s_id)
        layer1(nc, a, sem, sbuf, (sc, trp, cx, ms), ident, mhalf, whx, x1_dram, out)


def prologue(nc, a, sem, sbuf, psum, ident, mhalf, kst, v, q_dram, s_id, s_mh):
    sc, trp, cx, ms = psum
    NW = N // W
    banks = [sc[:, 0, 0:W], sc[:, 0, W:2 * W], sc[:, 1, 0:W], sc[:, 1, W:2 * W],
             trp[:, 0, :], trp[:, 1, :]]
    NBK = len(banks)
    with ExitStack() as ctx:
        xT = sbuf(ctx, "xT", [P, C, N])
        wk = sbuf(ctx, "wk", [P, C, D])
        wq = sbuf(ctx, "wq", [P, C, D])
        wv = sbuf(ctx, "wv", [P, C, D])
        bk = sbuf(ctx, "bk", [P, C])
        bq = sbuf(ctx, "bq", [P, C])
        bv = sbuf(ctx, "bv", [P, D])
        khi = sbuf(ctx, "k_hi", [P, G, N], F16)
        klo = sbuf(ctx, "k_lo", [P, G, N], F16)
        qhi = sbuf(ctx, "q_hi", [P, G, N], F16)
        qlo = sbuf(ctx, "q_lo", [P, G, N], F16)
        s_x = [sem(f"s_x{n}") for n in range(NW)]
        s_wk, s_wq, s_wv = sem("s_wk"), sem("s_wq"), sem("s_wv")
        s_pr, s_hi, s_lo, s_vd = sem("s_proj"), sem("s_hi"), sem("s_lo"), sem("s_vdone")
        s_kst, s_qdr = sem("s_kstack"), sem("s_qdram")

        jobs = [("k", g, n) for g in range(G) for n in range(NW)]
        jobs += [("q", g, n) for g in range(G) for n in range(NW)]
        jobs += [("v", r, 0) for r in range(KC // 2)]
        NKQ = 2 * G * NW
        block = ctx.enter_context(nc.Block())

        @block.sync
        def _(sp):
            sp.dma_start(wk[:, :, :], a["L0_gnn_WkT"].rearrange("(c p) m -> p c m", p=P)).then_inc(s_wk, 16)
            sp.dma_start(bk[:, :], a["L0_gnn_bk_cols"]).then_inc(s_wk, 16)
            for n in range(NW):
                sp.dma_start(xT[:, :, n * W:(n + 1) * W],
                             a["xT"].rearrange("(c p) n -> p c n", p=P)[:, :, n * W:(n + 1) * W]).then_inc(s_x[n], 16)
            sp.dma_start(wq[:, :, :], a["L0_gnn_WqT"].rearrange("(c p) m -> p c m", p=P)).then_inc(s_wq, 16)
            sp.dma_start(bq[:, :], a["L0_gnn_bq_cols"]).then_inc(s_wq, 16)
            sp.dma_start(wv[:, :, :], a["L0_gnn_WvT"].rearrange("(c p) m -> p c m", p=P)).then_inc(s_wv, 16)
            sp.dma_start(bv[:, :], a["L0_gnn_bv"].partition_broadcast(P)).then_inc(s_wv, 16)
            for g in range(G):
                sp.wait_ge(s_hi, NW * (g + 1))
                sp.wait_ge(s_lo, NW * (g + 1))
                for hh in range(HG):
                    for r in range(4):
                        src = khi if r % 2 == 0 else klo
                        sp.dma_start(kst[32 * r:32 * r + 32, g * HG + hh, :],
                                     src[DK * hh:DK * hh + DK, g, :]).then_inc(s_kst, 16)
            sp.wait_ge(s_hi, NKQ)
            sp.wait_ge(s_lo, NKQ)
            for part, src in enumerate((qhi, qlo)):
                sp.dma_start(q_dram[part].rearrange("(g p) n -> p g n", p=P), src[:, :, :]).then_inc(s_qdr, 16)
            sp.wait_ge(s_kst, 16 * G * HG * 4)
            sp.wait_ge(s_qdr, 32)

        @block.gpsimd
        def _(pool):
            nc.gpsimd.memset(ident[:, :], 0.0).then_inc(s_id, 1)
            nc.gpsimd.memset(mhalf[:, :], -0.5).then_inc(s_mh, 1)
            pool.wait_ge(s_id, 1)
            nc.gpsimd.affine_select(out=ident[:, :], in_=ident[:, :], compare_op=ALU.not_equal, fill=1.0,
                                    base=0, pattern=[[-1, P]], channel_multiplier=1).then_inc(s_id, 1)

        @block.tensor
        def _(pe):
            pe.wait_ge(s_wk, 32)
            for i, (what, g, n) in enumerate(jobs):
                bank = banks[i % NBK]
                if (what, g, n) == ("q", 0, 0):
                    pe.wait_ge(s_wq, 32)
                if (what, g, n) == ("v", 0, 0):
                    pe.wait_ge(s_wv, 32)
                if what == "k" and g == 0:
                    pe.wait_ge(s_x[n], 16)
                back = i - NBK
                if back >= 0:
                    if back < NKQ:
                        pe.wait_ge(s_lo, back + 1)
                    else:
                        pe.wait_ge(s_vd, back - NKQ + 1)
                if what in "kq":
                    w = wk if what == "k" else wq
                    for c in range(C):
                        mm = nc.tensor.matmul(bank, w[:, c, g * P:(g + 1) * P], xT[:, c, n * W:(n + 1) * W],
                                              start=(c == 0), stop=(c == C - 1))
                else:
                    for j in range(2):
                        r = 2 * g + j
                        for c in range(C):
                            mm = nc.tensor.matmul(bank[:, j * D:(j + 1) * D], xT[:, c, r * P:(r + 1) * P],
                                                  wv[:, c, :], start=(c == 0), stop=(c == C - 1))
                mm.then_inc(s_pr, 1)

        @block.scalar
        def _(act):
            for i, (what, g, n) in enumerate(jobs[:NKQ]):
                hi, b = (khi, bk) if what == "k" else (qhi, bq)
                act.wait_ge(s_pr, i + 1)
                if i == G * NW:
                    act.wait_ge(s_wq, 32)
                nc.scalar.activation(hi[:, g, n * W:(n + 1) * W], banks[i % NBK], ACT.Identity,
                                     bias=b[:, g:g + 1]).then_inc(s_hi, 1)

        @block.vector
        def _(dve):
            for i, (what, g, n) in enumerate(jobs):
                bank = banks[i % NBK]
                dve.wait_ge(s_pr, i + 1)
                if what == "v":
                    if g == 0:
                        dve.wait_ge(s_wv, 32)
                    for j in range(2):
                        add = nc.vector.tensor_tensor(v[:, 2 * g + j, :], bank[:, j * D:(j + 1) * D], bv[:, :], ALU.add)
                    add.then_inc(s_vd, 1)
                    continue
                hi, lo, b = (khi, klo, bk) if what == "k" else (qhi, qlo, bq)
                dve.wait_ge(s_hi, i + 1)
                nc.vector.scalar_tensor_tensor(out=lo[:, g, n * W:(n + 1) * W], in0=bank, scalar=b[:, g:g + 1],
                                               in1=hi[:, g, n * W:(n + 1) * W], op0=ALU.add,
                                               op1=ALU.subtract).then_inc(s_lo, 1)


def layer0(nc, a, sem, sbuf, psum, ident, mhalf, whx, kst, v, pb, msk, q_dram, x1_dram, s_id):
    sc, trp, cx, ms = psum
    MC = FF // P
    TAIL_USES = 13
    with ExitStack() as ctx:
        qst = sbuf(ctx, "q_stack", [P, H, QB], F16)
        pt = sbuf(ctx, "probs_T", [P, HG, KC, QB])
        adj_half = sbuf(ctx, "adj_half", [P, HALF], I32)
        adj_diag = sbuf(ctx, "adj_diag", [P, P], I32)
        ident_i = sbuf(ctx, "ident_i", [P, P], I32)
        wo = sbuf(ctx, "wo", [P, C, D])
        w1 = sbuf(ctx, "w1", [P, C, FF])
        w2 = sbuf(ctx, "w2", [P, MC, D])
        b1 = sbuf(ctx, "b1", [P, MC])
        rows = {n: sbuf(ctx, n, [P, D]) for n in
                ("bo", "b2", "ln1_g", "ln1_b", "ln2_g", "ln2_b", "n1_g", "n1_b")}
        wl = sbuf(ctx, "w_l1", [P, C, DK])
        sel = sbuf(ctx, "wh_select", [DK, DK + 2])
        xr = sbuf(ctx, "x_rows", [P, RB, D])
        ctxT = sbuf(ctx, "ctx_T", [P, G, QB])
        rdT = sbuf(ctx, "rden_T", [P, QB])
        rdw = sbuf(ctx, "rden_wide", [P, RB, HG, DK])
        h1 = sbuf(ctx, "h1", [P, RB, D])
        xr2 = sbuf(ctx, "ffn_rows", [P, RB, D])
        hT = sbuf(ctx, "h_T", [P, C, QB])
        reluT = sbuf(ctx, "relu_T", [P, MC // 2, QB])
        whT = reluT[0:DK, 0, :]
        nmax = sbuf(ctx, "neg_max", [P, PBUF, 2])
        rs = sbuf(ctx, "row_sum", [P, TPB])
        rd = sbuf(ctx, "rden", [P, RB * HG])
        st = sbuf(ctx, "ln_stats", [P, RB, 6])
        mv = sbuf(ctx, "ln_mv", [P, RB, 2])
        ve = sbuf(ctx, "ln_rstd", [P, RB])

        s_w = sem("s_weights")
        NWT = 16
        s_ii = sem("s_ident_i")
        s_q = [sem(f"s_q{g}") for g in range(G)]
        s_adj, s_dg = sem("s_adj_half"), sem("s_adj_diag")
        s_cvh, s_cvm = sem("s_half_converted"), sem("s_diag_mask")
        s_qk, s_ttr, s_exp, s_tr = sem("s_qk"), sem("s_max"), sem("s_exp"), sem("s_transposed")
        s_eva, s_evd = sem("s_evac_act"), sem("s_evac_dve")
        s_rd, s_rdw = sem("s_rden"), sem("s_rden_wide")
        s_pv, s_ctx = sem("s_pv"), sem("s_ctx")
        s_ms, s_mse = sem("s_misc_written"), sem("s_misc_read")
        s_xr, s_xb = sem("s_x_rows"), sem("s_x_plus_bo")
        s_bn, s_ag, s_ve, s_rstd = sem("s_bn"), sem("s_aggr"), sem("s_var_eps"), sem("s_rstd")
        s_cen, s_ln = sem("s_centered"), sem("s_layernorm")
        s_h1b, s_x1o = sem("s_h1_plus_b2"), sem("s_x1_stored")

        def misc_base(sb):
            return 2 + TAIL_USES * (sb - 1) if not (isinstance(sb, int) and sb == 0) else 0

        def rden_use(sb, g, tail):
            return misc_base(sb) + ((7, -1)[g] if tail else 0)

        RDEN = {(0, 2): 1, (TPB // G + 1, 0): 0}

        block = ctx.enter_context(nc.Block())

        def looped(eng, body, tail):
            body(0, False, False)
            eng.wait_ge(s_w, 16 * NWT)
            with eng.Fori(1, NB - 1) as sb:
                body(sb, True, False)
            body(NB - 1, True, True)
            tail(NB)

        @block.sync
        def _(sp):
            hold = holder(sp, sem("s_hold_sp"))

            def load_q(sb, g):
                for r in range(4):
                    src = q_dram[r // 2, g * P:(g + 1) * P, bass.ds(sb * QB, QB)]
                    sp.dma_start(qst[32 * r:32 * r + 32, g * HG:(g + 1) * HG, :],
                                 src.rearrange("(h d) n -> d h n", d=DK)).then_inc(s_q[g], 16)

            def load_adj(sb, b, half):
                k = (sb * RB + b) * 2 + half
                wait(sp, s_cvh, k)
                hold()
                sp.dma_start(adj_half[:, :], a["adj"][bass.ds(sb * QB + b * P, P),
                                                      half * HALF:(half + 1) * HALF]).then_inc(s_adj, 16)

            def load_diag(sb, b):
                wait(sp, s_cvm, 2 * (sb * RB + b))
                hold()
                sp.dma_start(adj_diag[:, :], a["adj"][bass.ds(sb * QB + b * P, P),
                                                      bass.ds(sb * QB + b * P, P)]).then_inc(s_dg, 16)

            def load_x(sb):
                sp.dma_start(xr[:, :, :], a["x"][bass.ds(sb * QB, QB), :].rearrange("(b p) d -> p b d", p=P))\
                    .then_inc(s_xr, 16)

            def store_x1(of):
                sp.wait_ge(s_ln, 3 * of + 2)
                hold()
                sp.dma_start(x1_dram[bass.ds(of * QB, QB), :].rearrange("(b p) d -> p b d", p=P), h1[:, :, :])\
                    .then_inc(s_x1o, 16)

            sp.dma_start(ident_i[:, :], a["ident_i"]).then_inc(s_ii, 16)
            load_diag(0, 0)
            load_adj(0, 0, 0)
            load_q(0, 0)
            load_q(0, 1)
            load_adj(0, 0, 1)
            load_diag(0, 1)
            load_adj(0, 1, 0)
            load_adj(0, 1, 1)
            sp.dma_start(wo[:, :, :], a["L0_gnn_WoT"].rearrange("(c p) m -> p c m", p=P)).then_inc(s_w, 16)
            sp.dma_start(w1[:, :, :], a["L0_gnn_W1T"].rearrange("(c p) m -> p c m", p=P)).then_inc(s_w, 16)
            sp.dma_start(w2[:, :, :], a["L0_gnn_W2T"].rearrange("(c p) m -> p c m", p=P)).then_inc(s_w, 16)
            sp.dma_start(b1[:, :], a["L0_gnn_b1_cols"]).then_inc(s_w, 16)
            for n, src in (("bo", "L0_gnn_bo"), ("b2", "L0_gnn_b2"), ("ln1_g", "L0_gnn_ln1_g"),
                           ("ln1_b", "L0_gnn_ln1_b"), ("ln2_g", "L0_gnn_ln2_g"), ("ln2_b", "L0_gnn_ln2_b"),
                           ("n1_g", "L1_gnn_ln1_g"), ("n1_b", "L1_gnn_ln1_b")):
                sp.dma_start(rows[n][:, :], a[src].partition_broadcast(P)).then_inc(s_w, 16)
            sp.dma_start(wl[:, :, :], a["L1_gnn_W"].rearrange("(c p) m -> p c m", p=P)).then_inc(s_w, 16)
            sp.dma_start(sel[:, 0:DK], a["ident"][0:DK, 0:DK]).then_inc(s_w, 16)
            for j in range(2):
                sp.dma_start(sel[:, DK + j:DK + j + 1], a["L1_gnn_a"][j * DK:(j + 1) * DK, :]).then_inc(s_w, 16)

            def body(sb, tail, last):
                if tail:
                    sp.wait_ge(s_mse, misc_base(sb) + 1)
                    hold()
                load_x(sb)
                if not last:
                    load_diag(sb + 1, 0)
                    load_adj(sb + 1, 0, 0)
                    sp.wait_ge(s_qk, 2 * (TPB * sb + TPB // 2))
                    hold()
                    load_q(sb + 1, 0)
                    load_adj(sb + 1, 0, 1)
                if tail:
                    store_x1(sb - 1)
                if not last:
                    load_adj(sb + 1, 1, 0)
                    load_diag(sb + 1, 1)
                    load_adj(sb + 1, 1, 1)
                    sp.wait_ge(s_qk, 2 * (TPB * sb + TPB))
                    hold()
                    load_q(sb + 1, 1)

            looped(sp, body, lambda sb: store_x1(sb - 1))
            sp.wait_ge(s_x1o, 16 * NB)

        @block.gpsimd
        def _(pool):
            hold = holder(pool, sem("s_hold_pool"))

            def rstd(n):
                wait(pool, s_ag, RB * (n + 1))
                hold()
                nc.gpsimd.tensor_scalar(ve[:, :], mv[:, :, 1], EPS, None, ALU.add).then_inc(s_ve, 1)
                wait(pool, s_ve, n + 1)
                nc.gpsimd.tensor_tensor(ve[:, :], ve[:, :], mhalf[:, 0:RB], ALU.pow).then_inc(s_rstd, 1)

            def add_b2(of):
                wait(pool, s_ln, 3 * of + 1)
                for i in range(RB):
                    add = nc.gpsimd.tensor_tensor(xr2[:, i, :], h1[:, i, :], rows["b2"][:, :], ALU.add)
                add.then_inc(s_h1b, 1)

            def add_bo(sb):
                wait(pool, s_xr, 16 * (sb + 1))
                for i in range(RB):
                    add = nc.gpsimd.tensor_tensor(xr[:, i, :], xr[:, i, :], rows["bo"][:, :], ALU.add)
                add.then_inc(s_xb, 1)

            pool.wait_ge(s_w, 16 * NWT)

            def tail_alone(sb):
                rstd(3 * (sb - 1))
                add_b2(sb - 1)
                rstd(3 * (sb - 1) + 1)
                rstd(3 * (sb - 1) + 2)

            def body(sb, tail, last):
                if not tail:
                    add_bo(sb)
                    return
                rstd(3 * (sb - 1))
                add_bo(sb)
                add_b2(sb - 1)
                rstd(3 * (sb - 1) + 1)
                rstd(3 * (sb - 1) + 2)

            looped(pool, body, tail_alone)

        @block.tensor
        def _(pe):
            def scores(tile, t, sb, half):
                g, b, hh = tile_of(t)
                if t % (RB * HG) == 0 and half == 0:
                    wait(pe, s_q[g], 64 * (sb + 1))
                wait(pe, s_ttr, 2 * (tile - 1) + half + 1)
                for j in range(HALF // W):
                    mm = nc.tensor.matmul(sc[:, half, j * W:(j + 1) * W],
                                          qst[:, g * HG + hh, b * P:(b + 1) * P],
                                          kst[:, g * HG + hh, half * HALF + j * W:half * HALF + (j + 1) * W],
                                          start=True, stop=True)
                mm.then_inc(s_qk, 1)

            def transposes(tile, t, j):
                if j == 0:
                    wait(pe, s_exp, tile + 1)
                if j == 3:
                    wait(pe, s_evd, tile + 1)
                else:
                    wait(pe, s_eva, 3 * tile + j - 1)
                for i in range(4):
                    k = 4 * j + i
                    mm = nc.tensor.transpose(trp[:, j % 2, i * P:(i + 1) * P],
                                             pb[:, t % PBUF, k * P:(k + 1) * P], ident[:, :])
                mm.then_inc(s_tr, 1)

            def turn_rden(u, n):
                wait(pe, s_mse, u)
                wait(pe, s_rdw, n + 1)
                for b in range(RB):
                    mm = nc.tensor.transpose(ms[:, b * P:(b + 1) * P],
                                             rdw[:, b, :, :].rearrange("p h d -> p (h d)"), ident[:, :])
                mm.then_inc(s_ms, 1)

            def pv(tile, g, n, part):
                if part == 0:
                    wait(pe, s_eva, 3 * tile)
                    wait(pe, s_evd, tile)
                    wait(pe, s_ctx, n)
                for k in range(4 * part, 4 * part + 4):
                    for hh in range(HG):
                        mm = nc.tensor.matmul(cx[DK * hh:DK * hh + DK, 0:QB],
                                              v[:, k, g * P + DK * hh:g * P + DK * hh + DK],
                                              pt[:, hh, k, :], start=(k == 0), stop=(k == KC - 1))
                if part == 3:
                    mm.then_inc(s_pv, 1)

            def attention_out(u, of):
                wait(pe, s_mse, u)
                wait(pe, s_ctx, G * (of + 1))
                for b in range(RB):
                    for g in range(G):
                        mm = nc.tensor.matmul(ms[:, b * D:(b + 1) * D], ctxT[:, g, b * P:(b + 1) * P],
                                              wo[:, g, :], start=(g == 0), stop=(g == G - 1))
                mm.then_inc(s_ms, 1)

            def turn_rows(u, n, buf):
                wait(pe, s_mse, u)
                wait(pe, s_ln, n)
                for c in range(C):
                    for b in range(RB):
                        mm = nc.tensor.transpose(ms[:, c * QB + b * P:c * QB + (b + 1) * P],
                                                 buf[:, b, c * P:(c + 1) * P], ident[:, :])
                mm.then_inc(s_ms, 1)

            def ffn_up(u, m0):
                wait(pe, s_mse, u)
                for m in (m0, m0 + 1):
                    for c in range(C):
                        mm = nc.tensor.matmul(ms[:, (m - m0) * QB:(m - m0 + 1) * QB], w1[:, c, m * P:(m + 1) * P],
                                              hT[:, c, :], start=(c == 0), stop=(c == C - 1))
                mm.then_inc(s_ms, 1)

            def ffn_down(u, part, b):
                if b == 0:
                    wait(pe, s_mse, u)
                for m in range(MC // 2):
                    mm = nc.tensor.matmul(ms[:, b * D:(b + 1) * D], reluT[:, m, b * P:(b + 1) * P],
                                          w2[:, part * MC // 2 + m, :], start=(m == 0), stop=(m == MC // 2 - 1))
                if b == RB - 1:
                    mm.then_inc(s_ms, 1)

            def project_l1(u):
                wait(pe, s_mse, u)
                for c in range(C):
                    mm = nc.tensor.matmul(ms[0:DK, 0:QB], wl[:, c, :], hT[:, c, :], start=(c == 0), stop=(c == C - 1))
                mm.then_inc(s_ms, 1)

            def split_l1(u):
                wait(pe, s_mse, u)
                for b in range(RB):
                    mm = nc.tensor.matmul(ms[:, b * (DK + 2):(b + 1) * (DK + 2)], whT[:, b * P:(b + 1) * P],
                                          sel[:, :], start=True, stop=True)
                mm.then_inc(s_ms, 1)

            def tail_step(t, j, of, base, rden):
                if (t, j) == (1, 3):
                    attention_out(base + 0, of)
                elif (t, j) == (4, 1):
                    turn_rows(base + 1, 3 * of + 1, h1)
                elif (t, j) == (5, 1):
                    ffn_up(base + 2, 0)
                elif (t, j) == (6, 1):
                    ffn_up(base + 3, 2)
                elif t == 7 and j % 2 == 1:
                    ffn_down(base + 4, 0, j // 2)
                elif (t, j) == (8, 0):
                    ffn_up(base + 5, 4)
                elif (t, j) == (8, 2):
                    ffn_up(base + 6, 6)
                elif t == 9 and j % 2 == 1:
                    ffn_down(base + rden + 7, 1, j // 2)
                elif (t, j) == (13, 1):
                    turn_rows(base + rden + 8, 3 * of + 3, xr2)
                elif (t, j) == (14, 1):
                    project_l1(base + rden + 9)
                elif (t, j) == (15, 1):
                    split_l1(base + rden + 10)

            pe.wait_ge(s_id, 2)
            for tile in range(2):
                for half in range(2):
                    scores(tile, tile, 0, half)

            def body(sb, tail, last):
                for t in range(TPB):
                    tile = TPB * sb + t
                    for j in range(4):
                        if j % 2 == 0 and not (last and t + 2 >= TPB):
                            scores(tile + 2, (t + 2) % TPB, sb + (t + 2) // TPB, j // 2)
                        if t == TPB // G:
                            pv(tile, 0, G * sb, j)
                        elif t == 0 and tail:
                            pv(tile, 1, G * sb - 1, j)
                        transposes(tile, t, j)
                        g = RDEN.get((t, j))
                        if g is not None and (g == 0 or tail):
                            turn_rden(rden_use(sb, g, tail), G * sb - g)
                        if tail:
                            tail_step(t, j, sb - 1, misc_base(sb), 1)

            def tail_alone(sb):
                turn_rden(rden_use(sb, 1, True), G * sb - 1)
                for j in range(4):
                    pv(TPB * sb, 1, G * sb - 1, j)
                for t in range(TPB):
                    for j in range(4):
                        tail_step(t, j, sb - 1, misc_base(sb), 0)

            looped(pe, body, tail_alone)

        @block.vector
        def _(dve):
            hold = holder(dve, sem("s_hold_dve"))

            def reduce_half(tile, t, half, sb):
                g, b, hh = tile_of(t)
                slot = t % PBUF
                wait(dve, s_qk, 2 * tile + half + 1)
                if half == 0:
                    wait(dve, s_tr, 4 * (tile - PBUF + 1))
                    if g == 0 and hh == 0:
                        wait(dve, s_cvm, 2 * (RB * sb + b) + 2)
                else:
                    wait(dve, s_ttr, 2 * tile + 1)
                hold()
                nc.vector.tensor_tensor_reduce(
                    out=pb[:, slot, half * HALF:(half + 1) * HALF], in0=sc[:, half, :],
                    in1=msk[:, b, half * HALF:(half + 1) * HALF], scale=-SCALE,
                    scalar=BIG if half == 0 else nmax[:, slot, 0:1], op0=ALU.add, op1=ALU.min,
                    accum_out=nmax[:, slot, half:half + 1]).then_inc(s_ttr, 1)

            def evacuate(tile, t):
                g, b, hh = tile_of(t)
                wait(dve, s_tr, 4 * tile + 2)
                nc.vector.tensor_copy(pt[:, hh, 4:8, b * P:(b + 1) * P],
                                      trp[:, 1, :].rearrange("p (k q) -> p k q", k=4)).then_inc(s_evd, 1)

            def convert(sb, b, half):
                k = sb * RB + b
                wait(dve, s_adj, 16 * (2 * k + half + 1))
                hold()
                nc.vector.tensor_scalar(msk[:, b, half * HALF:(half + 1) * HALF], adj_half[:, :], 0, NEG,
                                        ALU.is_equal, ALU.mult).then_inc(s_cvh, 1)

            def convert_diag(sb, b):
                k = sb * RB + b
                wait(dve, s_dg, 16 * (k + 1))
                hold()
                nc.vector.tensor_tensor(adj_diag[:, :], adj_diag[:, :], ident_i[:, :], ALU.add).then_inc(s_cvm, 1)
                wait(dve, s_cvh, 2 * k + 2)
                wait(dve, s_cvm, 2 * k + 1)
                hold()
                nc.vector.tensor_scalar(msk[:, b, bass.ds(sb * QB + b * P, P)], adj_diag[:, :], 0, NEG,
                                        ALU.is_equal, ALU.mult).then_inc(s_cvm, 1)

            def mask_ahead(t, sb):
                b = 0 if t < 14 else 1
                if t in (10, 11, 14, 15):
                    wait(dve, s_ttr, 2 * (TPB * (sb - 1) + TPB // 2 + (b + 1) * HG))
                    convert(sb, b, t % 2)
                elif t == 12:
                    convert_diag(sb, 0)

            def widen_rden(tile, g, n):
                wait(dve, s_exp, tile)
                nc.vector.reciprocal(rd[:, :], rs[:, g * RB * HG:(g + 1) * RB * HG]).then_inc(s_rd, 1)
                wait(dve, s_rd, n + 1)
                for b in range(RB):
                    cp = nc.vector.tensor_copy(
                        rdw[:, b, :, :], rd[:, b * HG:(b + 1) * HG].unsqueeze(2).to_broadcast([P, HG, DK]))
                cp.then_inc(s_rdw, 1)

            def scale_ctx(g, n, u):
                wait(dve, s_pv, n + 1)
                wait(dve, s_mse, u + 1)
                nc.vector.tensor_tensor(ctxT[:, g, :], cx[:, 0:QB], rdT[:, :], ALU.mult).then_inc(s_ctx, 1)

            def statistics(n, buf):
                for i in range(RB):
                    nc.vector.bn_stats(st[:, i, :], buf[:, i, :]).then_inc(s_bn, 1)
                wait(dve, s_bn, RB * (n + 1))
                hold()
                for i in range(RB):
                    nc.vector.bn_aggr(mv[:, i, :], st[:, i, :]).then_inc(s_ag, 1)

            def center(n, dst, buf, g):
                wait(dve, s_ag, RB * (n + 1))
                hold()
                for i in range(RB):
                    nc.vector.scalar_tensor_tensor(out=dst[:, i, :], in0=buf[:, i, :], scalar=mv[:, i, 0:1],
                                                   in1=rows[g][:, :], op0=ALU.subtract, op1=ALU.mult)\
                        .then_inc(s_cen, 1)

            def finish(n, buf, b):
                wait(dve, s_rstd, n + 1)
                wait(dve, s_cen, RB * (n + 1))
                hold()
                for i in range(RB):
                    op = nc.vector.scalar_tensor_tensor(out=buf[:, i, :], in0=buf[:, i, :], scalar=ve[:, i:i + 1],
                                                        in1=rows[b][:, :], op0=ALU.mult, op1=ALU.add)
                op.then_inc(s_ln, 1)

            LATE = (2, 8, 10)
            msv = ms[:, :].rearrange("p (b d) -> p b d", b=RB)

            def tail_step(t, of, base, rden):
                if t == 2:
                    wait(dve, s_ms, base + 1)
                    wait(dve, s_xb, of + 1)
                    wait(dve, s_x1o, 16 * of)
                    nc.vector.tensor_tensor(h1[:, :, :], msv, xr[:, :, :], ALU.add).then_inc(s_mse, 1)
                    wait(dve, s_mse, base + 1)
                    statistics(3 * of, h1)
                    center(3 * of, h1, h1, "ln1_g")
                elif t == 3:
                    finish(3 * of, h1, "ln1_b")
                elif t in (8, 10):
                    u = base + (4 if t == 8 else rden + 7)
                    wait(dve, s_ms, u + 1)
                    wait(dve, s_h1b, of + 1)
                    nc.vector.tensor_tensor(xr2[:, :, :], msv, xr2[:, :, :], ALU.add).then_inc(s_mse, 1)
                    if t == 10:
                        wait(dve, s_mse, u + 1)
                        statistics(3 * of + 1, xr2)
                        center(3 * of + 1, h1, xr2, "ln2_g")
                elif t == 11:
                    finish(3 * of + 1, h1, "ln2_b")
                    wait(dve, s_ln, 3 * of + 2)
                    statistics(3 * of + 2, h1)
                    center(3 * of + 2, xr2, h1, "n1_g")
                elif t == 12:
                    finish(3 * of + 2, xr2, "n1_b")
                elif t == 14:
                    u = base + rden + 9
                    wait(dve, s_ms, u + 1)
                    nc.vector.tensor_copy(whT, ms[0:DK, 0:QB]).then_inc(s_mse, 1)
                elif t == 15:
                    u = base + rden + 10
                    wait(dve, s_ms, u + 1)
                    nc.vector.tensor_copy(whx[:, bass.ds(of * RB, RB), :],
                                          ms[:, 0:RB * (DK + 2)].rearrange("p (b d) -> p b d", b=RB))\
                        .then_inc(s_mse, 1)

            dve.wait_ge(s_ii, 16)
            convert(0, 0, 0)
            convert(0, 0, 1)
            convert_diag(0, 0)
            reduce_half(0, 0, 0, 0)
            reduce_half(0, 0, 1, 0)
            reduce_half(1, 1, 0, 0)
            reduce_half(1, 1, 1, 0)
            convert(0, 1, 0)
            convert(0, 1, 1)

            def body(sb, tail, last):
                for t in range(TPB):
                    tile = TPB * sb + t
                    if t == 0:
                        convert_diag(sb, 1)
                    if t == 0 and tail:
                        widen_rden(tile, 1, G * sb - 1)
                    if t == TPB // G:
                        widen_rden(tile, 0, G * sb)
                    if tail and t in LATE:
                        tail_step(t, sb - 1, misc_base(sb), 1)
                    ahead = not (last and t + 2 >= TPB)
                    if ahead:
                        reduce_half(tile + 2, (t + 2) % TPB, 0, sb + (t + 2) // TPB)
                    if t == 1 and tail:
                        scale_ctx(1, G * sb - 1, rden_use(sb, 1, tail))
                    evacuate(tile, t)
                    if t == TPB // G + 1:
                        scale_ctx(0, G * sb, rden_use(sb, 0, tail))
                    if tail and t not in LATE + (15,):
                        tail_step(t, sb - 1, misc_base(sb), 1)
                    if ahead:
                        reduce_half(tile + 2, (t + 2) % TPB, 1, sb + (t + 2) // TPB)
                    if tail and t == 15:
                        tail_step(t, sb - 1, misc_base(sb), 1)
                    if not last:
                        mask_ahead(t, sb + 1)

            def tail_alone(sb):
                widen_rden(TPB * sb, 1, G * sb - 1)
                scale_ctx(1, G * sb - 1, rden_use(sb, 1, True))
                for t in range(TPB):
                    tail_step(t, sb - 1, misc_base(sb), 0)

            looped(dve, body, tail_alone)

        @block.scalar
        def _(act):
            def exponentiate(tile, t):
                slot = t % PBUF
                wait(act, s_ttr, 2 * tile + 2)
                nc.scalar.activation(pb[:, slot, :], pb[:, slot, :], ACT.Exp, bias=nmax[:, slot, 1:2], scale=-1.0,
                                     accum_out=rs[:, t:t + 1]).then_inc(s_exp, 1)

            def evacuate(tile, t, j):
                g, b, hh = tile_of(t)
                wait(act, s_tr, 4 * tile + j + 1)
                nc.scalar.activation(pt[:, hh, 4 * j:4 * j + 4, b * P:(b + 1) * P],
                                     trp[:, j % 2, :].rearrange("p (k q) -> p k q", k=4), ACT.Copy)\
                    .then_inc(s_eva, 1)

            def copy_rden(u, n):
                wait(act, s_ms, u + 1)
                wait(act, s_ctx, n)
                nc.scalar.activation(rdT[:, :], ms[:, 0:QB], ACT.Copy).then_inc(s_mse, 1)

            def turned(u):
                wait(act, s_ms, u + 1)
                nc.scalar.activation(hT[:, :, :], ms[:, :].rearrange("p (c q) -> p c q", c=C), ACT.Copy)\
                    .then_inc(s_mse, 1)

            def relu(u, m0):
                wait(act, s_ms, u + 1)
                for i in range(2):
                    r = nc.scalar.activation(reluT[:, (m0 + i) % (MC // 2), :], ms[:, i * QB:(i + 1) * QB],
                                             ACT.Relu, bias=b1[:, m0 + i:m0 + i + 1])
                r.then_inc(s_mse, 1)

            def tail_step(t, j, of, base, rden):
                if (t, j) == (4, 2):
                    turned(base + 1)
                elif (t, j) == (5, 2):
                    relu(base + 2, 0)
                elif (t, j) == (6, 2):
                    relu(base + 3, 2)
                elif (t, j) == (8, 1):
                    relu(base + 5, 4)
                elif (t, j) == (8, 3):
                    relu(base + 6, 6)
                elif (t, j) == (13, 2):
                    turned(base + rden + 8)

            exponentiate(0, 0)

            def body(sb, tail, last):
                for t in range(TPB):
                    tile = TPB * sb + t
                    nxt = (tile + 1, (t + 1) % TPB)
                    ahead = not (last and t + 1 >= TPB)
                    evacuate(tile, t, 0)
                    if ahead:
                        exponentiate(*nxt)
                    for j in (1, 2, 3):
                        if tail:
                            tail_step(t, j, sb - 1, misc_base(sb), 1)
                        if j > 1:
                            evacuate(tile, t, j)
                        g = RDEN.get((t, j - 1))
                        if g is not None and (g == 0 or tail):
                            copy_rden(rden_use(sb, g, tail), G * sb - g)

            def tail_alone(sb):
                copy_rden(rden_use(sb, 1, True), G * sb - 1)
                for t in range(TPB):
                    for j in (1, 2, 3):
                        tail_step(t, j, sb - 1, misc_base(sb), 0)

            looped(act, body, tail_alone)


def layer1(nc, a, sem, sbuf, psum, ident, mhalf, whx, x1_dram, out):
    sc, trp, cx, ms = psum
    MC = HID // P
    banks = [sc[:, 0, 0:W], sc[:, 0, W:2 * W], sc[:, 1, 0:W], sc[:, 1, W:2 * W]]
    pair = [ms, cx]
    with ExitStack() as ctx:
        fdb = sbuf(ctx, "f_dst_rows", [P, N])
        fs2 = sbuf(ctx, "f_src_low", [P, KC])
        x1 = sbuf(ctx, "x1_rows", [P, KC, D])
        pb = sbuf(ctx, "probs_l1", [P, 3, N])
        low = sbuf(ctx, "leaky_low", [P, 2, N])
        msk = sbuf(ctx, "mask_l1", [P, N], BF16)
        adj = sbuf(ctx, "adj_l1", [P, 2, N], I32)
        pt = sbuf(ctx, "probs_T_l1", [P, 2, KC, SQ])
        fc = sbuf(ctx, "fc4", [P, D])
        fc1 = sbuf(ctx, "fc1", [P, C, HID])
        fc2 = sbuf(ctx, "fc2", [P, MC, D])
        fb1 = sbuf(ctx, "fc1_b", [P, MC])
        rows = {n: sbuf(ctx, "l1_" + n, [P, D]) for n in ("fc_b", "g", "b", "fc2_b")}
        hp = sbuf(ctx, "h_prime_T", [P, SQ])
        h2 = sbuf(ctx, "h2", [P, ST, D])
        h2T = sbuf(ctx, "h2_T", [P, C, SQ])
        geluT = sbuf(ctx, "gelu_T", [P, MC, SQ])
        yo = sbuf(ctx, "out_rows", [P, ST, D])
        nmax = sbuf(ctx, "neg_max_l1", [P, KC])
        rs = sbuf(ctx, "row_sum_l1", [P, KC])
        rd = sbuf(ctx, "rden_l1", [P, KC])
        st = sbuf(ctx, "stats_l1", [P, ST, 6])
        mv = sbuf(ctx, "mv_l1", [P, ST, 2])
        ve = sbuf(ctx, "rstd_l1", [P, ST])

        s_w, s_x = sem("s_l1_weights"), sem("s_l1_x1")
        NWT = 11
        s_adj = [sem(f"s_l1_adj{i}") for i in range(2)]
        s_fdt, s_fdb, s_fs = sem("s_l1_fd_turned"), sem("s_l1_fd"), sem("s_l1_fs_low")
        s_cv, s_low, s_lr, s_max, s_exp = (sem("s_l1_" + n) for n in ("mask", "low", "leaky", "max", "exp"))
        s_tr, s_eva, s_evd = (sem("s_l1_" + n) for n in ("turned", "evac_act", "evac_dve"))
        s_pv, s_hp, s_fc, s_x2, s_rd = (sem("s_l1_" + n) for n in ("pv", "h_prime", "fc", "x2", "rden"))
        s_xb, s_bn, s_ag, s_ve, s_rstd = (sem("s_l1_" + n) for n in ("x1b", "bn", "aggr", "ve", "rstd"))
        s_nrm, s_g, s_gb, s_ht, s_hte = (sem("s_l1_" + n) for n in ("norm", "gain", "ln", "h2_turned", "h2T"))
        s_up, s_ge, s_dn, s_yc, s_y = (sem("s_l1_" + n) for n in ("up", "gelu", "down", "y_copied", "y"))
        s_x2b, s_out = sem("s_l1_x2b"), sem("s_l1_out")

        block = ctx.enter_context(nc.Block())

        def steps():
            for t in range(KC + 2 * ST):
                s = t // ST
                u = s - 1 if 0 < s <= NS else None
                w = s - 2 if s > 1 else None
                yield t, t % ST, u, w

        @block.sync
        def _(sp):
            def load_adj(t):
                wait(sp, s_cv, t - 1)
                sp.dma_start(adj[:, t % 2, :], a["adj"][t * P:(t + 1) * P, :]).then_inc(s_adj[t % 2], 16)

            load_adj(0)
            load_adj(1)
            sp.dma_start(x1[:, :, :], x1_dram.rearrange("(t p) d -> p t d", p=P)).then_inc(s_x, 16)
            load_adj(2)
            for i in range(4):
                sp.dma_start(fc[DK * i:DK * i + DK, :], a["L1_gnn_fc_wT"]).then_inc(s_w, 16)
            sp.dma_start(rows["fc_b"][:, :], a["L1_gnn_fc_b"].partition_broadcast(P)).then_inc(s_w, 16)
            sp.dma_start(rows["g"][:, :], a["L1_gnn_ln2_g"].partition_broadcast(P)).then_inc(s_w, 16)
            sp.dma_start(rows["b"][:, :], a["L1_gnn_ln2_b"].partition_broadcast(P)).then_inc(s_w, 16)
            sp.dma_start(rows["fc2_b"][:, :], a["L1_gnn_fc2_b"].partition_broadcast(P)).then_inc(s_w, 16)
            sp.dma_start(fc1[:, :, :], a["L1_gnn_fc1_wT"].rearrange("(c p) m -> p c m", p=P)).then_inc(s_w, 16)
            sp.dma_start(fc2[:, :, :], a["L1_gnn_fc2_wT"].rearrange("(c p) m -> p c m", p=P)).then_inc(s_w, 16)
            sp.dma_start(fb1[:, :], a["L1_gnn_fc1_b_cols"]).then_inc(s_w, 16)
            for t in range(3, KC):
                load_adj(t)
            for w in range(NS):
                sp.wait_ge(s_y, w + 1)
                sp.dma_start(out[w * SQ:(w + 1) * SQ, :].rearrange("(t p) d -> p t d", p=P), yo[:, :, :])\
                    .then_inc(s_out, 16)
            sp.wait_ge(s_out, 16 * NS)

        @block.gpsimd
        def _(pool):
            def add_row(s, name, done):
                for i in range(ST):
                    t = s * ST + i
                    add = nc.gpsimd.tensor_tensor(x1[:, t, :], x1[:, t, :], rows[name][:, :], ALU.add)
                add.then_inc(done, 1)

            def layernorm(u):
                wait(pool, s_ag, ST * (u + 1))
                nc.gpsimd.tensor_scalar(ve[:, :], mv[:, :, 1], EPS, None, ALU.add).then_inc(s_ve, 1)
                wait(pool, s_ve, u + 1)
                nc.gpsimd.tensor_tensor(ve[:, :], ve[:, :], mhalf[:, 0:ST], ALU.pow).then_inc(s_rstd, 1)
                wait(pool, s_rstd, u + 1)
                wait(pool, s_ht, u)
                for i in range(ST):
                    nc.gpsimd.tensor_scalar(h2[:, i, :], x1[:, u * ST + i, :], mv[:, i, 0:1], ve[:, i:i + 1],
                                            ALU.subtract, ALU.mult).then_inc(s_nrm, 1)
                for i in range(ST):
                    wait(pool, s_nrm, ST * u + i + 1)
                    nc.gpsimd.tensor_tensor(h2[:, i, :], h2[:, i, :], rows["g"][:, :], ALU.mult).then_inc(s_g, 1)
                for i in range(ST):
                    wait(pool, s_g, ST * u + i + 1)
                    nc.gpsimd.tensor_tensor(h2[:, i, :], h2[:, i, :], rows["b"][:, :], ALU.add).then_inc(s_gb, 1)

            def add_residual(w):
                wait(pool, s_x2b, w + 1)
                wait(pool, s_yc, 2 * (w + 1))
                for i in range(ST):
                    add = nc.gpsimd.tensor_tensor(yo[:, i, :], yo[:, i, :], x1[:, w * ST + i, :], ALU.add)
                add.then_inc(s_y, 1)

            nc.gpsimd.tensor_scalar(fs2[:, :], whx[:, :, DK], 0.2, None, ALU.mult).then_inc(s_fs, 1)
            pool.wait_ge(s_w, 16 * NWT)
            pool.wait_ge(s_x, 16)
            add_row(0, "fc_b", s_xb)
            for s in range(NS + 2):
                if s + 1 < NS:
                    add_row(s + 1, "fc_b", s_xb)
                if 0 < s <= NS:
                    layernorm(s - 1)
                    add_row(s - 1, "fc2_b", s_x2b)
                if s > 1:
                    add_residual(s - 2)

        @block.tensor
        def _(pe):
            def transposes(t, j):
                if j == 0:
                    wait(pe, s_exp, t + 1)
                if j == 3:
                    wait(pe, s_evd, t + 1)
                else:
                    wait(pe, s_eva, 3 * t + j - 1)
                for m in range(4):
                    k = 4 * j + m
                    mm = nc.tensor.transpose(trp[:, j % 2, m * P:(m + 1) * P], pb[:, t % 3, k * P:(k + 1) * P],
                                             ident[:, :])
                mm.then_inc(s_tr, 1)

            def pv(u):
                wait(pe, s_eva, 3 * ST * (u + 1))
                wait(pe, s_evd, ST * (u + 1))
                wait(pe, s_yc, 2 * (u - 1))
                for k in range(KC):
                    c = k % 4
                    mm = nc.tensor.matmul(cx[DK * c:DK * c + DK, :], whx[:, k, 0:DK], pt[:, u % 2, k, :],
                                          start=(k < 4), stop=(k >= KC - 4))
                mm.then_inc(s_pv, 1)

            def project(u):
                pe.wait_ge(s_w, 16 * NWT)
                wait(pe, s_hp, u + 1)
                wait(pe, s_yc, 2 * (u - 1))
                for m in range(ST):
                    mm = nc.tensor.matmul(pair[m // 2][:, (m % 2) * D:(m % 2 + 1) * D], hp[:, m * P:(m + 1) * P],
                                          fc[:, :], start=True, stop=True)
                    mm.then_inc(s_fc, 1)

            def turn_h2(u):
                wait(pe, s_gb, ST * (u + 1))
                wait(pe, s_ge, MC * u)
                for c in range(C):
                    for i in range(ST):
                        mm = nc.tensor.transpose(banks[c][:, i * P:(i + 1) * P], h2[:, i, c * P:(c + 1) * P],
                                                 ident[:, :])
                mm.then_inc(s_ht, 1)

            def up(w, m):
                wait(pe, s_hte, C * (w + 1))
                wait(pe, s_ge, MC * w)
                for c in range(C):
                    mm = nc.tensor.matmul(banks[m], fc1[:, c, m * P:(m + 1) * P], h2T[:, c, :],
                                          start=(c == 0), stop=(c == C - 1))
                mm.then_inc(s_up, 1)

            def down(w, i):
                wait(pe, s_ge, MC * (w + 1))
                wait(pe, s_x2, ST * min(w + 2, NS))
                for m in range(MC):
                    mm = nc.tensor.matmul(pair[i // 2][:, (i % 2) * D:(i % 2 + 1) * D],
                                          geluT[:, m, i * P:(i + 1) * P], fc2[:, m, :],
                                          start=(m == 0), stop=(m == MC - 1))
                mm.then_inc(s_dn, 1)

            for k in range(KC):
                mm = nc.tensor.transpose(banks[k // 4][:, (k % 4) * P:(k % 4 + 1) * P],
                                         whx[:, k, DK + 1:DK + 2].to_broadcast([P, P]), ident[:, :])
                if k % 4 == 3:
                    mm.then_inc(s_fdt, 1)

            for t, r, u, w in steps():
                for j in range(4):
                    if t < KC:
                        transposes(t, j)
                    if w is not None:
                        if (r, j) in UP:
                            up(w, UP[r, j])
                        if (r, j) in DOWN:
                            down(w, DOWN[r, j])
                    if u is not None:
                        if (r, j) == (0, 1):
                            pv(u)
                        elif (r, j) == (1, 1):
                            project(u)
                        elif (r, j) == (3, 3):
                            turn_h2(u)

        @block.scalar
        def _(act):
            def exponentiate(t):
                wait(act, s_max, t + 1)
                nc.scalar.activation(pb[:, t % 3, :], pb[:, t % 3, :], ACT.Exp, bias=nmax[:, t:t + 1], scale=-1.0,
                                     accum_out=rs[:, t:t + 1]).then_inc(s_exp, 1)

            def leaky_low(t):
                wait(act, s_lr, t - 1)
                nc.scalar.activation(low[:, t % 2, :], fdb[:, :], ACT.Identity, bias=fs2[:, t:t + 1], scale=0.2)\
                    .then_inc(s_low, 1)

            def evacuate(t, j):
                wait(act, s_tr, 4 * t + j + 1)
                if t % ST == 0:
                    wait(act, s_pv, t // ST - 1)
                nc.scalar.activation(pt[:, (t // ST) % 2, 4 * j:4 * j + 4, (t % ST) * P:(t % ST + 1) * P],
                                     trp[:, j % 2, :].rearrange("p (k q) -> p k q", k=4), ACT.Copy)\
                    .then_inc(s_eva, 1)

            for j in range(4):
                act.wait_ge(s_fdt, j + 1)
                nc.scalar.activation(fdb[:, j * W:(j + 1) * W], banks[j], ACT.Copy).then_inc(s_fdb, 1)
            act.wait_ge(s_fs, 1)
            act.wait_ge(s_fdb, 4)
            leaky_low(0)
            leaky_low(1)
            exponentiate(0)
            leaky_low(2)
            for t, r, u, w in steps():
                if t < KC:
                    evacuate(t, 0)
                if t + 1 < KC:
                    exponentiate(t + 1)
                if t < KC:
                    evacuate(t, 2)
                    evacuate(t, 3)
                if u is not None and r == 0:
                    wait(act, s_pv, u + 1)
                    wait(act, s_fc, ST * u)
                    nc.scalar.activation(hp[:, :], cx[:, :], ACT.Copy).then_inc(s_hp, 1)
                if w is not None and r == 1:
                    act.wait_ge(s_w, 16 * NWT)
                    wait(act, s_dn, ST * w)
                    wait(act, s_up, MC * (w + 1))
                    for m in range(MC):
                        nc.scalar.activation(geluT[:, m, :], banks[m], ACT.Gelu, bias=fb1[:, m:m + 1])\
                            .then_inc(s_ge, 1)
                if w is not None and r == 3:
                    wait(act, s_out, 16 * w)
                    for i in range(2):
                        wait(act, s_dn, ST * w + 2 * i + 2)
                        nc.scalar.activation(yo[:, 2 * i:2 * i + 2, :],
                                             pair[i][:, :].rearrange("p (b d) -> p b d", b=2), ACT.Copy)\
                            .then_inc(s_yc, 1)
                if u is not None and r == 3:
                    wait(act, s_ht, u + 1)
                    wait(act, s_up, MC * u)
                    for c in range(C):
                        nc.scalar.activation(h2T[:, c, :], banks[c], ACT.Copy).then_inc(s_hte, 1)
                if t + 3 < KC:
                    leaky_low(t + 3)

        @block.vector
        def _(dve):
            def leaky(t):
                wait(dve, s_low, t + 1)
                wait(dve, s_tr, 4 * (t - 2))
                nc.vector.scalar_tensor_tensor(out=pb[:, t % 3, :], in0=fdb[:, :], scalar=whx[:, t, DK:DK + 1],
                                               in1=low[:, t % 2, :], op0=ALU.add, op1=ALU.max).then_inc(s_lr, 1)

            def mask(t):
                wait(dve, s_adj[t % 2], 16 * (t // 2 + 1))
                wait(dve, s_max, t)
                nc.vector.tensor_scalar(msk[:, :], adj[:, t % 2, :], 0, NEG, ALU.is_le, ALU.mult).then_inc(s_cv, 1)

            def reduce(t):
                wait(dve, s_lr, t + 1)
                wait(dve, s_cv, t + 1)
                nc.vector.tensor_tensor_reduce(out=pb[:, t % 3, :], in0=pb[:, t % 3, :], in1=msk[:, :],
                                               scale=-1.0, scalar=BIG, op0=ALU.add, op1=ALU.min,
                                               accum_out=nmax[:, t:t + 1]).then_inc(s_max, 1)

            def residual(u):
                wait(dve, s_exp, ST * (u + 1))
                nc.vector.reciprocal(rd[:, u * ST:(u + 1) * ST], rs[:, u * ST:(u + 1) * ST]).then_inc(s_rd, 1)
                wait(dve, s_rd, u + 1)
                wait(dve, s_xb, u + 1)
                for i in range(ST):
                    t = u * ST + i
                    wait(dve, s_fc, u * ST + 2 * (i // 2) + 2)
                    nc.vector.scalar_tensor_tensor(out=x1[:, t, :], in0=pair[i // 2][:, (i % 2) * D:(i % 2 + 1) * D],
                                                   scalar=rd[:, t:t + 1], in1=x1[:, t, :], op0=ALU.mult,
                                                   op1=ALU.add).then_inc(s_x2, 1)
                for i in range(ST):
                    wait(dve, s_x2, ST * u + i + 1)
                    nc.vector.bn_stats(st[:, i, :], x1[:, u * ST + i, :]).then_inc(s_bn, 1)
                wait(dve, s_nrm, ST * u)
                for i in range(ST):
                    wait(dve, s_bn, ST * u + i + 1)
                    nc.vector.bn_aggr(mv[:, i, :], st[:, i, :]).then_inc(s_ag, 1)

            dve.wait_ge(s_fdb, 4)
            for t in range(2):
                mask(t)
                leaky(t)
                reduce(t)
            for t, r, u, w in steps():
                if t + 2 < KC:
                    mask(t + 2)
                if t < KC:
                    wait(dve, s_tr, 4 * t + 2)
                    if t % ST == 0:
                        wait(dve, s_pv, t // ST - 1)
                    nc.vector.tensor_copy(pt[:, (t // ST) % 2, 4:8, (t % ST) * P:(t % ST + 1) * P],
                                          trp[:, 1, :].rearrange("p (k q) -> p k q", k=4)).then_inc(s_evd, 1)
                if t + 2 < KC:
                    leaky(t + 2)
                    reduce(t + 2)
                if u is not None and r == 1:
                    residual(u)


UP = {(0, 0): 0, (1, 0): 1, (1, 2): 2, (1, 3): 3}
DOWN = {(2, 1): 0, (2, 3): 1, (3, 0): 2, (3, 2): 3}


TRANSPOSED = ("L0_gnn_Wq", "L0_gnn_Wk", "L0_gnn_Wv", "L0_gnn_Wo", "L0_gnn_W1", "L0_gnn_W2",
              "L1_gnn_fc_w", "L1_gnn_fc1_w", "L1_gnn_fc2_w")
COLUMNS = ("L0_gnn_bq", "L0_gnn_bk", "L0_gnn_b1", "L1_gnn_fc1_b")
AS_IS = ("x", "adj", "L0_gnn_bv", "L0_gnn_bo", "L0_gnn_b2",
         "L0_gnn_ln1_g", "L0_gnn_ln1_b", "L0_gnn_ln2_g", "L0_gnn_ln2_b", "L1_gnn_W", "L1_gnn_a",
         "L1_gnn_fc_b", "L1_gnn_ln1_g", "L1_gnn_ln1_b", "L1_gnn_ln2_g", "L1_gnn_ln2_b",
         "L1_gnn_fc2_b")


def kernel(**inputs):
    import concourse.bacc as bacc
    from concourse.bass_utils import run_bass_kernel_spmd

    host = {n: np.ascontiguousarray(inputs[n]) for n in AS_IS}
    host.update({n + "T": np.ascontiguousarray(np.asarray(inputs[n]).T) for n in ("x",) + TRANSPOSED})
    for n in COLUMNS:
        host[n + "_cols"] = np.ascontiguousarray(np.asarray(inputs[n]).reshape(-1, P).T)
    host["ident"] = np.eye(P, dtype=np.float32)
    host["ident_i"] = np.eye(P, dtype=np.int32)
    nc = bacc.Bacc("TRN2", target_bir_lowering=False, num_devices=1)
    aps = {n: nc.dram_tensor(f"in_{n}", x.shape, mybir.dt.from_np(x.dtype), kind="ExternalInput").ap()
           for n, x in host.items()}
    out = nc.dram_tensor("out_rows_dram", (N, D), F32, kind="ExternalOutput").ap()
    build(nc, aps, out)
    r = run_bass_kernel_spmd(nc, [{f"in_{n}": x for n, x in host.items()}], core_ids=[0])
    return r.results[0]["out_rows_dram"]
```

```python
from contextlib import ExitStack

import numpy as np

import concourse.bass as bass
from concourse import mybir

ALU = mybir.AluOpType
ACT = mybir.ActivationFunctionType
F32 = mybir.dt.float32
F16 = mybir.dt.float16
BF16 = mybir.dt.bfloat16
I32 = mybir.dt.int32

P = 128
N, D = 2048, 256
H = 8
DK = D // H
HG = P // DK
G = H // HG
C = D // P
FF = 1024
HID = 512
KC = N // P
QB = 256
NB = N // QB
RB = QB // P
TPB = G * RB * HG
HALF = N // 2
W = 512
PBUF = 4
NEG = -2.0 ** 100
EPS = 1e-5
SCALE = 1.0 / float(np.sqrt(np.float32(DK)))
BIG = 3.0e38
SQ = 512
NS = N // SQ
ST = SQ // P


WO_AT = [(1, 1), (1, 3)]
UP_AT = [(4, 1), (4, 3), (5, 1), (5, 3), (9, 1), (9, 3), (10, 1), (10, 3)]
DOWN_AT = [(6, 1), (6, 3), (7, 1), (7, 3), (11, 1), (11, 3), (12, 1), (12, 3)]


def wait(eng, sem, value):
    if isinstance(value, int) and value <= 0:
        return
    eng.wait_ge(sem, value)


def holder(eng, sem):
    return lambda: eng.sem_inc(sem, 1)


def tile_of(t):
    return t // (RB * HG), (t % (RB * HG)) // HG, t % HG


def build(nc, a, out):
    x1_dram = nc.dram_tensor("x1_scratch", (N, D), F32, kind="Internal").ap()
    q_dram = nc.dram_tensor("q_scratch", (2, D, N), F16, kind="Internal").ap()

    with ExitStack() as whole:
        def sem(name):
            return whole.enter_context(nc.semaphore(name))

        def sbuf(ctx, name, shape, dt=F32):
            return ctx.enter_context(nc.sbuf_tensor(name, shape, dt))

        sc = whole.enter_context(nc.psum_tensor("score_ps", [P, 2, HALF], F32))
        trp = whole.enter_context(nc.psum_tensor("transpose_ps", [P, 2, W], F32))
        cx = whole.enter_context(nc.psum_tensor("context_ps", [P, W], F32))
        ms = whole.enter_context(nc.psum_tensor("misc_ps", [P, W], F32))

        ident = sbuf(whole, "ident", [P, P])
        mhalf = sbuf(whole, "minus_half", [P, 4])
        whx = sbuf(whole, "whx", [P, KC, DK + 2])

        s_id = sem("s_id")
        s_mh = sem("s_mh")

        with ExitStack() as l0:
            kst = sbuf(l0, "k_stack", [P, H, N], F16)
            v = sbuf(l0, "v", [P, KC, D])
            pb = sbuf(l0, "probs", [P, PBUF, N])
            msk = sbuf(l0, "mask", [P, RB, N], BF16)
            qst = sbuf(l0, "q_stack", [P, H, QB], F16)
            ident_i = sbuf(l0, "ident_i", [P, P], I32)
            adj_diag = sbuf(l0, "adj_diag", [P, P], I32)
            prologue(nc, a, sem, sbuf, (sc, trp, cx, ms), ident, mhalf, kst, v, msk, qst, ident_i, adj_diag,
                     q_dram, s_id, s_mh)
            layer0(nc, a, sem, sbuf, (sc, trp, cx, ms), ident, mhalf, whx, kst, v, pb, msk, qst, ident_i, adj_diag,
                   q_dram, x1_dram, s_id)
        layer1(nc, a, sem, sbuf, (sc, trp, cx, ms), ident, mhalf, whx, x1_dram, out)


def load_q_block(eng, q_dram, qst, sb, g, done):
    for r in range(4):
        src = q_dram[r // 2, g * P:(g + 1) * P, bass.ds(sb * QB, QB)]
        eng.dma_start(qst[32 * r:32 * r + 32, g * HG:(g + 1) * HG, :],
                      src.rearrange("(h d) n -> d h n", d=DK)).then_inc(done, 16)


def prologue(nc, a, sem, sbuf, psum, ident, mhalf, kst, v, msk, qst, ident_i, adj_diag, q_dram, s_id, s_mh):
    sc, trp, cx, ms = psum
    NW = N // W
    banks = [sc[:, 0, 0:W], sc[:, 0, W:2 * W], sc[:, 1, 0:W], sc[:, 1, W:2 * W],
             trp[:, 0, :], trp[:, 1, :]]
    NBK = len(banks)
    with ExitStack() as ctx:
        xT = sbuf(ctx, "xT", [P, C, N])
        wk = sbuf(ctx, "wk", [P, C, D])
        wq = sbuf(ctx, "wq", [P, C, D])
        wv = sbuf(ctx, "wv", [P, C, D])
        bk = sbuf(ctx, "bk", [P, C])
        bq = sbuf(ctx, "bq", [P, C])
        bv = sbuf(ctx, "bv", [P, D])
        khi = sbuf(ctx, "k_hi", [P, G, N], F16)
        klo = sbuf(ctx, "k_lo", [P, G, N], F16)
        qhi = sbuf(ctx, "q_hi", [P, G, N], F16)
        qlo = sbuf(ctx, "q_lo", [P, G, N], F16)
        adj = sbuf(ctx, "adj_block0", [P, RB, N], I32)
        diag = sbuf(ctx, "adj_diag_block0", [P, RB, P], I32)
        s_x = [sem(f"s_x{n}") for n in range(NW)]
        s_wk, s_wq, s_wv = sem("s_wk"), sem("s_wq"), sem("s_wv")
        s_pr, s_hi, s_lo, s_vd = sem("s_proj"), sem("s_hi"), sem("s_lo"), sem("s_vdone")
        s_kst, s_qdr, s_q0 = sem("s_kstack"), sem("s_qdram"), sem("s_q_block0")
        s_adj, s_ii, s_m0 = sem("s_adj_block0"), sem("s_ident_i"), sem("s_mask_block0")

        jobs = [("k", g, n) for g in range(G) for n in range(NW)]
        jobs += [("q", g, n) for g in range(G) for n in range(NW)]
        jobs += [("v", r, 0) for r in range(KC // 2)]
        NKQ = 2 * G * NW
        block = ctx.enter_context(nc.Block())

        @block.sync
        def _(sp):
            sp.dma_start(wk[:, :, :], a["L0_gnn_WkT"].rearrange("(c p) m -> p c m", p=P)).then_inc(s_wk, 16)
            sp.dma_start(bk[:, :], a["L0_gnn_bk_cols"]).then_inc(s_wk, 16)
            for n in range(NW):
                sp.dma_start(xT[:, :, n * W:(n + 1) * W],
                             a["xT"].rearrange("(c p) n -> p c n", p=P)[:, :, n * W:(n + 1) * W]).then_inc(s_x[n], 16)
            sp.dma_start(wq[:, :, :], a["L0_gnn_WqT"].rearrange("(c p) m -> p c m", p=P)).then_inc(s_wq, 16)
            sp.dma_start(bq[:, :], a["L0_gnn_bq_cols"]).then_inc(s_wq, 16)
            sp.dma_start(wv[:, :, :], a["L0_gnn_WvT"].rearrange("(c p) m -> p c m", p=P)).then_inc(s_wv, 16)
            sp.dma_start(bv[:, :], a["L0_gnn_bv"].partition_broadcast(P)).then_inc(s_wv, 16)
            sp.dma_start(ident_i[:, :], a["ident_i"]).then_inc(s_ii, 16)
            for b in range(RB):
                sp.dma_start(adj[:, b, :], a["adj"][b * P:(b + 1) * P, :]).then_inc(s_adj, 16)
                sp.dma_start(diag[:, b, :], a["adj"][b * P:(b + 1) * P, b * P:(b + 1) * P]).then_inc(s_adj, 16)
            for g in range(G):
                sp.wait_ge(s_hi, NW * (g + 1))
                sp.wait_ge(s_lo, NW * (g + 1))
                for hh in range(HG):
                    for r in range(4):
                        src = khi if r % 2 == 0 else klo
                        sp.dma_start(kst[32 * r:32 * r + 32, g * HG + hh, :],
                                     src[DK * hh:DK * hh + DK, g, :]).then_inc(s_kst, 16)
            sp.wait_ge(s_hi, NKQ)
            sp.wait_ge(s_lo, NKQ)
            for part, src in enumerate((qhi, qlo)):
                sp.dma_start(q_dram[part].rearrange("(g p) n -> p g n", p=P), src[:, :, :]).then_inc(s_qdr, 16)
            sp.wait_ge(s_qdr, 32)
            for g in range(G):
                load_q_block(sp, q_dram, qst, 0, g, s_q0)
            sp.wait_ge(s_kst, 16 * G * HG * 4)
            sp.wait_ge(s_q0, 64 * G)

        @block.gpsimd
        def _(pool):
            nc.gpsimd.memset(ident[:, :], 0.0).then_inc(s_id, 1)
            nc.gpsimd.memset(mhalf[:, :], -0.5).then_inc(s_mh, 1)
            pool.wait_ge(s_id, 1)
            nc.gpsimd.affine_select(out=ident[:, :], in_=ident[:, :], compare_op=ALU.not_equal, fill=1.0,
                                    base=0, pattern=[[-1, P]], channel_multiplier=1).then_inc(s_id, 1)

        @block.tensor
        def _(pe):
            pe.wait_ge(s_wk, 32)
            for i, (what, g, n) in enumerate(jobs):
                bank = banks[i % NBK]
                if (what, g, n) == ("q", 0, 0):
                    pe.wait_ge(s_wq, 32)
                if (what, g, n) == ("v", 0, 0):
                    pe.wait_ge(s_wv, 32)
                if what == "k" and g == 0:
                    pe.wait_ge(s_x[n], 16)
                back = i - NBK
                if back >= 0:
                    if back < NKQ:
                        pe.wait_ge(s_lo, back + 1)
                    else:
                        pe.wait_ge(s_vd, back - NKQ + 1)
                if what in "kq":
                    w = wk if what == "k" else wq
                    for c in range(C):
                        mm = nc.tensor.matmul(bank, w[:, c, g * P:(g + 1) * P], xT[:, c, n * W:(n + 1) * W],
                                              start=(c == 0), stop=(c == C - 1))
                else:
                    for j in range(2):
                        r = 2 * g + j
                        for c in range(C):
                            mm = nc.tensor.matmul(bank[:, j * D:(j + 1) * D], xT[:, c, r * P:(r + 1) * P],
                                                  wv[:, c, :], start=(c == 0), stop=(c == C - 1))
                mm.then_inc(s_pr, 1)

        @block.scalar
        def _(act):
            for i, (what, g, n) in enumerate(jobs[:NKQ]):
                hi, b = (khi, bk) if what == "k" else (qhi, bq)
                act.wait_ge(s_pr, i + 1)
                if i == G * NW:
                    act.wait_ge(s_wq, 32)
                nc.scalar.activation(hi[:, g, n * W:(n + 1) * W], banks[i % NBK], ACT.Identity,
                                     bias=b[:, g:g + 1]).then_inc(s_hi, 1)

        @block.vector
        def _(dve):
            def mask_block0(b):
                if b == 0:
                    dve.wait_ge(s_ii, 16)
                    dve.wait_ge(s_adj, 32 * RB)
                nc.vector.tensor_scalar(msk[:, b, :], adj[:, b, :], 0, NEG, ALU.is_equal, ALU.mult).then_inc(s_m0, 1)
                nc.vector.tensor_tensor(diag[:, b, :], diag[:, b, :], ident_i[:, :], ALU.add).then_inc(s_m0, 1)
                dve.wait_ge(s_m0, 3 * b + 2)
                nc.vector.tensor_scalar(msk[:, b, b * P:(b + 1) * P], diag[:, b, :], 0, NEG, ALU.is_equal,
                                        ALU.mult).then_inc(s_m0, 1)

            for i, (what, g, n) in enumerate(jobs):
                if what == "v" and g < RB:
                    mask_block0(g)
                bank = banks[i % NBK]
                dve.wait_ge(s_pr, i + 1)
                if what == "v":
                    if g == 0:
                        dve.wait_ge(s_wv, 32)
                    for j in range(2):
                        add = nc.vector.tensor_tensor(v[:, 2 * g + j, :], bank[:, j * D:(j + 1) * D], bv[:, :], ALU.add)
                    add.then_inc(s_vd, 1)
                    continue
                hi, lo, b = (khi, klo, bk) if what == "k" else (qhi, qlo, bq)
                dve.wait_ge(s_hi, i + 1)
                nc.vector.scalar_tensor_tensor(out=lo[:, g, n * W:(n + 1) * W], in0=bank, scalar=b[:, g:g + 1],
                                               in1=hi[:, g, n * W:(n + 1) * W], op0=ALU.add,
                                               op1=ALU.subtract).then_inc(s_lo, 1)


def layer0(nc, a, sem, sbuf, psum, ident, mhalf, whx, kst, v, pb, msk, qst, ident_i, adj_diag, q_dram, x1_dram, s_id):
    sc, trp, cx, ms = psum
    MC = FF // P
    TAIL_USES = 12
    with ExitStack() as ctx:
        pt = sbuf(ctx, "probs_T", [P, HG, KC, QB])
        adj_half = sbuf(ctx, "adj_half", [P, HALF], I32)
        wo = sbuf(ctx, "wo", [P, C, D])
        w1 = sbuf(ctx, "w1", [P, C, FF])
        w2 = sbuf(ctx, "w2", [P, MC, D])
        b1 = sbuf(ctx, "b1", [P, MC])
        rows = {n: sbuf(ctx, n, [P, D]) for n in
                ("bo", "b2", "ln1_g", "ln1_b", "ln2_g", "ln2_b", "n1_g", "n1_b")}
        wT = sbuf(ctx, "w_l1_T", [DK, D])
        wl = sbuf(ctx, "w_l1", [P, C, DK + 2])
        sel = sbuf(ctx, "wh_select", [DK, DK + 2])
        xr = sbuf(ctx, "x_rows", [P, RB, D])
        ctxT = sbuf(ctx, "ctx_T", [P, G, QB])
        rdT = sbuf(ctx, "rden_T", [P, QB])
        rdw = sbuf(ctx, "rden_wide", [P, RB, HG, DK])
        h1 = sbuf(ctx, "h1", [P, RB, D])
        xr2 = sbuf(ctx, "ffn_rows", [P, RB, D])
        hT = sbuf(ctx, "h_T", [P, C, QB])
        reluT = sbuf(ctx, "relu_T", [P, MC // 2, QB])
        nmax = sbuf(ctx, "neg_max", [P, PBUF, 2])
        rs = sbuf(ctx, "row_sum", [P, TPB])
        rd = sbuf(ctx, "rden", [P, RB * HG])
        st = sbuf(ctx, "ln_stats", [P, RB, 6])
        mv = sbuf(ctx, "ln_mv", [P, RB, 2])
        ve = sbuf(ctx, "ln_rstd", [P, RB])

        s_w = sem("s_weights")
        NWT = 12
        s_wl = sem("s_l1_w_loads")
        s_q = [sem(f"s_q{g}") for g in range(G)]
        s_adj, s_dg = sem("s_adj_half"), sem("s_adj_diag")
        s_cvh, s_cvm = sem("s_half_converted"), sem("s_diag_mask")
        s_qk, s_ttr, s_exp, s_tr = sem("s_qk"), sem("s_max"), sem("s_exp"), sem("s_transposed")
        s_eva, s_evd = sem("s_evac_act"), sem("s_evac_dve")
        s_rd, s_rdw = sem("s_rden"), sem("s_rden_wide")
        s_pv, s_ctx = sem("s_pv"), sem("s_ctx")
        s_ms, s_mse = sem("s_misc_written"), sem("s_misc_read")
        s_xr, s_xb = sem("s_x_rows"), sem("s_x_plus_bo")
        s_bn, s_ag, s_ve, s_rstd = sem("s_bn"), sem("s_aggr"), sem("s_var_eps"), sem("s_rstd")
        s_cen, s_ln = sem("s_centered"), sem("s_layernorm")
        s_h1b, s_x1o = sem("s_h1_plus_b2"), sem("s_x1_stored")

        def misc_base(sb):
            return 3 + TAIL_USES * (sb - 1) if not (isinstance(sb, int) and sb == 0) else 1

        def rden_use(sb, g, tail):
            return misc_base(sb) + ((5, -1)[g] if tail else 0)

        RDEN = {(0, 3): 1, (TPB // G, 3): 0}

        block = ctx.enter_context(nc.Block())

        def looped(eng, body, tail):
            body(0, False, False, False)
            eng.wait_ge(s_w, 16 * NWT)
            body(1, True, False, False)
            with eng.Fori(2, NB - 1) as sb:
                body(sb, True, True, False)
            body(NB - 1, True, True, True)
            tail(NB)

        @block.sync
        def _(sp):
            hold = holder(sp, sem("s_hold_sp"))

            def load_q(sb, g):
                load_q_block(sp, q_dram, qst, sb, g, s_q[g])

            def load_adj(sb, b, half):
                k = ((sb - 1) * RB + b) * 2 + half
                wait(sp, s_cvh, k)
                hold()
                sp.dma_start(adj_half[:, :], a["adj"][bass.ds(sb * QB + b * P, P),
                                                      half * HALF:(half + 1) * HALF]).then_inc(s_adj, 16)

            def load_diag(sb, b):
                wait(sp, s_cvm, 2 * ((sb - 1) * RB + b))
                hold()
                sp.dma_start(adj_diag[:, :], a["adj"][bass.ds(sb * QB + b * P, P),
                                                      bass.ds(sb * QB + b * P, P)]).then_inc(s_dg, 16)

            def load_x(sb):
                sp.dma_start(xr[:, :, :], a["x"][bass.ds(sb * QB, QB), :].rearrange("(b p) d -> p b d", p=P))\
                    .then_inc(s_xr, 16)

            def store_x1(of):
                sp.wait_ge(s_ln, 3 * of + 2)
                hold()
                sp.dma_start(x1_dram[bass.ds(of * QB, QB), :].rearrange("(b p) d -> p b d", p=P), h1[:, :, :])\
                    .then_inc(s_x1o, 16)

            load_diag(1, 0)
            load_adj(1, 0, 0)
            sp.dma_start(wT[:, :], a["L1_gnn_WT"]).then_inc(s_wl, 16)
            sp.dma_start(sel[:, 0:DK], a["ident"][0:DK, 0:DK]).then_inc(s_wl, 16)
            for j in range(2):
                sp.dma_start(sel[:, DK + j:DK + j + 1], a["L1_gnn_a"][j * DK:(j + 1) * DK, :]).then_inc(s_wl, 16)
            sp.dma_start(wo[:, :, :], a["L0_gnn_WoT"].rearrange("(c p) m -> p c m", p=P)).then_inc(s_w, 16)
            sp.dma_start(w1[:, :, :], a["L0_gnn_W1T"].rearrange("(c p) m -> p c m", p=P)).then_inc(s_w, 16)
            sp.dma_start(w2[:, :, :], a["L0_gnn_W2T"].rearrange("(c p) m -> p c m", p=P)).then_inc(s_w, 16)
            sp.dma_start(b1[:, :], a["L0_gnn_b1_cols"]).then_inc(s_w, 16)
            for n, src in (("bo", "L0_gnn_bo"), ("b2", "L0_gnn_b2"), ("ln1_g", "L0_gnn_ln1_g"),
                           ("ln1_b", "L0_gnn_ln1_b"), ("ln2_g", "L0_gnn_ln2_g"), ("ln2_b", "L0_gnn_ln2_b"),
                           ("n1_g", "L1_gnn_ln1_g"), ("n1_b", "L1_gnn_ln1_b")):
                sp.dma_start(rows[n][:, :], a[src].partition_broadcast(P)).then_inc(s_w, 16)

            def body(sb, tail, end, last):
                if tail:
                    sp.wait_ge(s_mse, misc_base(sb) + 1)
                    hold()
                load_x(sb)
                if not last:
                    if not (isinstance(sb, int) and sb == 0):
                        load_diag(sb + 1, 0)
                        load_adj(sb + 1, 0, 0)
                    sp.wait_ge(s_qk, 2 * (TPB * sb + TPB // 2))
                    hold()
                    load_q(sb + 1, 0)
                    load_adj(sb + 1, 0, 1)
                if tail:
                    store_x1(sb - 1)
                if not last:
                    load_adj(sb + 1, 1, 0)
                    load_diag(sb + 1, 1)
                    load_adj(sb + 1, 1, 1)
                    sp.wait_ge(s_qk, 2 * (TPB * sb + TPB))
                    hold()
                    load_q(sb + 1, 1)

            looped(sp, body, lambda sb: store_x1(sb - 1))
            sp.wait_ge(s_x1o, 16 * NB)

        @block.gpsimd
        def _(pool):
            hold = holder(pool, sem("s_hold_pool"))

            def rstd(n):
                wait(pool, s_ag, RB * (n + 1))
                hold()
                nc.gpsimd.tensor_scalar(ve[:, :], mv[:, :, 1], EPS, None, ALU.add).then_inc(s_ve, 1)
                wait(pool, s_ve, n + 1)
                nc.gpsimd.tensor_tensor(ve[:, :], ve[:, :], mhalf[:, 0:RB], ALU.pow).then_inc(s_rstd, 1)

            def add_b2(of):
                wait(pool, s_ln, 3 * of + 1)
                for i in range(RB):
                    add = nc.gpsimd.tensor_tensor(xr2[:, i, :], h1[:, i, :], rows["b2"][:, :], ALU.add)
                add.then_inc(s_h1b, 1)

            def add_bo(sb):
                wait(pool, s_xr, 16 * (sb + 1))
                for i in range(RB):
                    add = nc.gpsimd.tensor_tensor(xr[:, i, :], xr[:, i, :], rows["bo"][:, :], ALU.add)
                add.then_inc(s_xb, 1)

            pool.wait_ge(s_w, 16 * NWT)

            def tail_alone(sb):
                rstd(3 * (sb - 1))
                add_b2(sb - 1)
                rstd(3 * (sb - 1) + 1)
                rstd(3 * (sb - 1) + 2)

            def body(sb, tail, end, last):
                if not tail:
                    add_bo(sb)
                    return
                rstd(3 * (sb - 1))
                add_bo(sb)
                add_b2(sb - 1)
                rstd(3 * (sb - 1) + 1)
                rstd(3 * (sb - 1) + 2)

            looped(pool, body, tail_alone)

        @block.tensor
        def _(pe):
            def scores(tile, t, sb, half):
                g, b, hh = tile_of(t)
                if t % (RB * HG) == 0 and half == 0:
                    wait(pe, s_q[g], 64 * sb)
                wait(pe, s_ttr, 2 * (tile - 1) + half + 1)
                for j in range(HALF // W):
                    mm = nc.tensor.matmul(sc[:, half, j * W:(j + 1) * W],
                                          qst[:, g * HG + hh, b * P:(b + 1) * P],
                                          kst[:, g * HG + hh, half * HALF + j * W:half * HALF + (j + 1) * W],
                                          start=True, stop=True)
                mm.then_inc(s_qk, 1)

            def transposes(tile, t, j):
                if j == 0:
                    wait(pe, s_exp, tile + 1)
                if j == 3:
                    wait(pe, s_evd, tile + 1)
                else:
                    wait(pe, s_eva, 3 * tile + j - 1)
                for i in range(4):
                    k = 4 * j + i
                    mm = nc.tensor.transpose(trp[:, j % 2, i * P:(i + 1) * P],
                                             pb[:, t % PBUF, k * P:(k + 1) * P], ident[:, :])
                mm.then_inc(s_tr, 1)

            def turn_rden(u, n):
                wait(pe, s_mse, u)
                wait(pe, s_rdw, n + 1)
                for b in range(RB):
                    mm = nc.tensor.transpose(ms[:, b * P:(b + 1) * P],
                                             rdw[:, b, :, :].rearrange("p h d -> p (h d)"), ident[:, :])
                mm.then_inc(s_ms, 1)

            def pv(tile, g, n, part):
                if part == 0:
                    wait(pe, s_eva, 3 * tile)
                    wait(pe, s_evd, tile)
                    wait(pe, s_ctx, n)
                for k in range(4 * part, 4 * part + 4):
                    for hh in range(HG):
                        mm = nc.tensor.matmul(cx[DK * hh:DK * hh + DK, 0:QB],
                                              v[:, k, g * P + DK * hh:g * P + DK * hh + DK],
                                              pt[:, hh, k, :], start=(k == 0), stop=(k == KC - 1))
                if part == 3:
                    mm.then_inc(s_pv, 1)

            def attention_out(u, of, b):
                if b == 0:
                    wait(pe, s_mse, u)
                    wait(pe, s_ctx, G * (of + 1))
                for g in range(G):
                    mm = nc.tensor.matmul(ms[:, b * D:(b + 1) * D], ctxT[:, g, b * P:(b + 1) * P],
                                          wo[:, g, :], start=(g == 0), stop=(g == G - 1))
                if b == RB - 1:
                    mm.then_inc(s_ms, 1)

            def turn_rows(u, n, buf):
                wait(pe, s_mse, u)
                wait(pe, s_ln, n)
                for c in range(C):
                    for b in range(RB):
                        mm = nc.tensor.transpose(ms[:, c * QB + b * P:c * QB + (b + 1) * P],
                                                 buf[:, b, c * P:(c + 1) * P], ident[:, :])
                mm.then_inc(s_ms, 1)

            def ffn_up(u, m):
                if m % 2 == 0:
                    wait(pe, s_mse, u)
                for c in range(C):
                    mm = nc.tensor.matmul(ms[:, (m % 2) * QB:(m % 2 + 1) * QB], w1[:, c, m * P:(m + 1) * P],
                                          hT[:, c, :], start=(c == 0), stop=(c == C - 1))
                if m % 2 == 1:
                    mm.then_inc(s_ms, 1)

            def ffn_down(u, part, i):
                b = i // 2
                if i == 0:
                    wait(pe, s_mse, u)
                for m in (2 * (i % 2), 2 * (i % 2) + 1):
                    mm = nc.tensor.matmul(ms[:, b * D:(b + 1) * D], reluT[:, m, b * P:(b + 1) * P],
                                          w2[:, part * MC // 2 + m, :], start=(m == 0), stop=(m == MC // 2 - 1))
                if i == 3:
                    mm.then_inc(s_ms, 1)

            def extend_w():
                pe.wait_ge(s_wl, 64)
                for c in range(C):
                    mm = nc.tensor.matmul(ms[:, c * (DK + 2):(c + 1) * (DK + 2)], wT[:, c * P:(c + 1) * P],
                                          sel[:, :], start=True, stop=True)
                mm.then_inc(s_ms, 1)

            def project_l1(u):
                wait(pe, s_mse, u)
                for b in range(RB):
                    for c in range(C):
                        mm = nc.tensor.matmul(ms[:, b * (DK + 2):(b + 1) * (DK + 2)], hT[:, c, b * P:(b + 1) * P],
                                              wl[:, c, :], start=(c == 0), stop=(c == C - 1))
                mm.then_inc(s_ms, 1)

            def tail_step(t, j, of, base, rden):
                if (t, j) in WO_AT:
                    attention_out(base, of, WO_AT.index((t, j)))
                elif (t, j) == (3, 3):
                    turn_rows(base + 1, 3 * of + 1, h1)
                elif (t, j) in UP_AT:
                    m = UP_AT.index((t, j))
                    ffn_up(base + (2, 3, 5 + rden, 6 + rden)[m // 2], m)
                elif (t, j) in DOWN_AT:
                    i = DOWN_AT.index((t, j))
                    ffn_down(base + (4, 7 + rden)[i // 4], i // 4, i % 4)

            def tail_end(t, j, of, use):
                if (t, j) == (0, 1):
                    turn_rows(use, 3 * of + 3, xr2)
                elif (t, j) == (0, 2):
                    project_l1(use + 1)

            pe.wait_ge(s_id, 2)
            for tile in range(2):
                for half in range(2):
                    scores(tile, tile, 0, half)

            def body(sb, tail, end, last):
                for t in range(TPB):
                    tile = TPB * sb + t
                    for j in range(4):
                        ahead = not (last and t + 2 >= TPB)
                        if j == 0 and ahead:
                            scores(tile + 2, (t + 2) % TPB, sb + (t + 2) // TPB, 0)
                        if t == TPB // G:
                            pv(tile, 0, G * sb, j)
                        elif t == 0 and tail:
                            pv(tile, 1, G * sb - 1, j)
                        transposes(tile, t, j)
                        if j == 1 and ahead:
                            scores(tile + 2, (t + 2) % TPB, sb + (t + 2) // TPB, 1)
                        if end:
                            tail_end(t, j, sb - 2, misc_base(sb) - 3)
                        g = RDEN.get((t, j))
                        if g is not None and (g == 0 or tail):
                            turn_rden(rden_use(sb, g, tail), G * sb - g)
                        if tail:
                            tail_step(t, j, sb - 1, misc_base(sb), 1)
                        elif (t, j) == (4, 3):
                            extend_w()

            def tail_alone(sb):
                base = misc_base(sb)
                for j in range(4):
                    pv(TPB * sb, 1, G * sb - 1, j)
                    tail_end(0, j, sb - 2, base - 3)
                turn_rden(rden_use(sb, 1, True), G * sb - 1)
                for t in range(TPB):
                    for j in range(4):
                        tail_step(t, j, sb - 1, base, 0)
                for j in range(4):
                    tail_end(0, j, sb - 1, base + 8)

            looped(pe, body, tail_alone)

        @block.vector
        def _(dve):
            hold = holder(dve, sem("s_hold_dve"))

            def reduce_half(tile, t, half, sb):
                g, b, hh = tile_of(t)
                slot = t % PBUF
                wait(dve, s_qk, 2 * tile + half + 1)
                if half == 0:
                    wait(dve, s_tr, 4 * (tile - PBUF + 1))
                    if g == 0 and hh == 0 and not (isinstance(sb, int) and sb == 0):
                        wait(dve, s_cvm, 2 * (RB * (sb - 1) + b) + 2)
                else:
                    wait(dve, s_ttr, 2 * tile + 1)
                hold()
                nc.vector.tensor_tensor_reduce(
                    out=pb[:, slot, half * HALF:(half + 1) * HALF], in0=sc[:, half, :],
                    in1=msk[:, b, half * HALF:(half + 1) * HALF], scale=-SCALE,
                    scalar=BIG if half == 0 else nmax[:, slot, 0:1], op0=ALU.add, op1=ALU.min,
                    accum_out=nmax[:, slot, half:half + 1]).then_inc(s_ttr, 1)

            def evacuate(tile, t):
                g, b, hh = tile_of(t)
                wait(dve, s_tr, 4 * tile + 2)
                nc.vector.tensor_copy(pt[:, hh, 4:8, b * P:(b + 1) * P],
                                      trp[:, 1, :].rearrange("p (k q) -> p k q", k=4)).then_inc(s_evd, 1)

            def convert(sb, b, half):
                k = (sb - 1) * RB + b
                wait(dve, s_adj, 16 * (2 * k + half + 1))
                hold()
                nc.vector.tensor_scalar(msk[:, b, half * HALF:(half + 1) * HALF], adj_half[:, :], 0, NEG,
                                        ALU.is_equal, ALU.mult).then_inc(s_cvh, 1)

            def convert_diag(sb, b):
                k = (sb - 1) * RB + b
                wait(dve, s_dg, 16 * (k + 1))
                hold()
                nc.vector.tensor_tensor(adj_diag[:, :], adj_diag[:, :], ident_i[:, :], ALU.add).then_inc(s_cvm, 1)
                wait(dve, s_cvh, 2 * k + 2)
                wait(dve, s_cvm, 2 * k + 1)
                hold()
                nc.vector.tensor_scalar(msk[:, b, bass.ds(sb * QB + b * P, P)], adj_diag[:, :], 0, NEG,
                                        ALU.is_equal, ALU.mult).then_inc(s_cvm, 1)

            def mask_ahead(t, sb):
                if t in (10, 11):
                    wait(dve, s_ttr, 2 * (TPB * (sb - 1) + TPB // 2 + HG))
                    convert(sb, 0, t - 10)
                elif t == 12:
                    convert_diag(sb, 0)
                elif t == 15:
                    wait(dve, s_ttr, 2 * TPB * sb)
                    convert(sb, 1, 0)

            def widen_rden(tile, g, n):
                wait(dve, s_exp, tile)
                nc.vector.reciprocal(rd[:, :], rs[:, g * RB * HG:(g + 1) * RB * HG]).then_inc(s_rd, 1)
                wait(dve, s_rd, n + 1)
                for b in range(RB):
                    cp = nc.vector.tensor_copy(
                        rdw[:, b, :, :], rd[:, b * HG:(b + 1) * HG].unsqueeze(2).to_broadcast([P, HG, DK]))
                cp.then_inc(s_rdw, 1)

            def scale_ctx(g, n, u):
                wait(dve, s_pv, n + 1)
                wait(dve, s_mse, u + 1)
                nc.vector.tensor_tensor(ctxT[:, g, :], cx[:, 0:QB], rdT[:, :], ALU.mult).then_inc(s_ctx, 1)

            def statistics(n, buf):
                for i in range(RB):
                    nc.vector.bn_stats(st[:, i, :], buf[:, i, :]).then_inc(s_bn, 1)
                wait(dve, s_bn, RB * (n + 1))
                hold()
                for i in range(RB):
                    nc.vector.bn_aggr(mv[:, i, :], st[:, i, :]).then_inc(s_ag, 1)

            def center(n, dst, buf, g):
                wait(dve, s_ag, RB * (n + 1))
                hold()
                for i in range(RB):
                    nc.vector.scalar_tensor_tensor(out=dst[:, i, :], in0=buf[:, i, :], scalar=mv[:, i, 0:1],
                                                   in1=rows[g][:, :], op0=ALU.subtract, op1=ALU.mult)\
                        .then_inc(s_cen, 1)

            def finish(n, buf, b):
                wait(dve, s_rstd, n + 1)
                wait(dve, s_cen, RB * (n + 1))
                hold()
                for i in range(RB):
                    op = nc.vector.scalar_tensor_tensor(out=buf[:, i, :], in0=buf[:, i, :], scalar=ve[:, i:i + 1],
                                                        in1=rows[b][:, :], op0=ALU.mult, op1=ALU.add)
                op.then_inc(s_ln, 1)

            msv = ms[:, :].rearrange("p (b d) -> p b d", b=RB)

            def tail_step(t, late, of, base, rden):
                if (t, late) == (2, 0):
                    wait(dve, s_ms, base + 1)
                    wait(dve, s_xb, of + 1)
                    wait(dve, s_x1o, 16 * of)
                    nc.vector.tensor_tensor(h1[:, :, :], msv, xr[:, :, :], ALU.add).then_inc(s_mse, 1)
                    wait(dve, s_mse, base + 1)
                    statistics(3 * of, h1)
                elif (t, late) == (2, 1):
                    center(3 * of, h1, h1, "ln1_g")
                elif (t, late) == (3, 0):
                    finish(3 * of, h1, "ln1_b")
                elif (t, late) in ((8, 0), (13, 0)):
                    u = base + (4 if t == 8 else rden + 7)
                    wait(dve, s_ms, u + 1)
                    wait(dve, s_h1b, of + 1)
                    nc.vector.tensor_tensor(xr2[:, :, :], msv, xr2[:, :, :], ALU.add).then_inc(s_mse, 1)
                    if t == 13:
                        wait(dve, s_mse, u + 1)
                        statistics(3 * of + 1, xr2)
                elif (t, late) == (13, 1):
                    center(3 * of + 1, h1, xr2, "ln2_g")
                    finish(3 * of + 1, h1, "ln2_b")
                elif (t, late) == (14, 0):
                    wait(dve, s_ln, 3 * of + 2)
                    statistics(3 * of + 2, h1)
                    center(3 * of + 2, xr2, h1, "n1_g")
                elif (t, late) == (14, 1):
                    finish(3 * of + 2, xr2, "n1_b")

            def tail_end(of, use):
                wait(dve, s_ms, use + 2)
                nc.vector.tensor_copy(whx[:, bass.ds(of * RB, RB), :],
                                      ms[:, 0:RB * (DK + 2)].rearrange("p (b d) -> p b d", b=RB)).then_inc(s_mse, 1)

            reduce_half(0, 0, 0, 0)
            reduce_half(0, 0, 1, 0)
            reduce_half(1, 1, 0, 0)
            reduce_half(1, 1, 1, 0)

            def body(sb, tail, end, last):
                for t in range(TPB):
                    tile = TPB * sb + t
                    if t == 0 and not (isinstance(sb, int) and sb == 0):
                        convert(sb, 1, 1)
                        convert_diag(sb, 1)
                    if t == 0 and tail:
                        widen_rden(tile, 1, G * sb - 1)
                    if t == TPB // G:
                        widen_rden(tile, 0, G * sb)
                    if t == 1 and tail:
                        scale_ctx(1, G * sb - 1, rden_use(sb, 1, tail))
                    ahead = not (last and t + 2 >= TPB)
                    if ahead:
                        reduce_half(tile + 2, (t + 2) % TPB, 0, sb + (t + 2) // TPB)
                    evacuate(tile, t)
                    if tail:
                        tail_step(t, 0, sb - 1, misc_base(sb), 1)
                    if ahead:
                        reduce_half(tile + 2, (t + 2) % TPB, 1, sb + (t + 2) // TPB)
                    if t == TPB // G + 1:
                        scale_ctx(0, G * sb, rden_use(sb, 0, tail))
                    if end and t == 0:
                        tail_end(sb - 2, misc_base(sb) - 3)
                    if tail:
                        tail_step(t, 1, sb - 1, misc_base(sb), 1)
                    elif t == 5:
                        dve.wait_ge(s_ms, 1)
                        nc.vector.tensor_copy(wl[:, :, :], ms[:, 0:C * (DK + 2)].rearrange("p (c d) -> p c d", c=C))\
                            .then_inc(s_mse, 1)
                    if not last:
                        mask_ahead(t, sb + 1)

            def tail_alone(sb):
                widen_rden(TPB * sb, 1, G * sb - 1)
                tail_end(sb - 2, misc_base(sb) - 3)
                scale_ctx(1, G * sb - 1, rden_use(sb, 1, True))
                for t in range(TPB):
                    for late in range(2):
                        tail_step(t, late, sb - 1, misc_base(sb), 0)
                tail_end(sb - 1, misc_base(sb) + 8)

            looped(dve, body, tail_alone)

        @block.scalar
        def _(act):
            def exponentiate(tile, t):
                slot = t % PBUF
                wait(act, s_ttr, 2 * tile + 2)
                nc.scalar.activation(pb[:, slot, :], pb[:, slot, :], ACT.Exp, bias=nmax[:, slot, 1:2], scale=-1.0,
                                     accum_out=rs[:, t:t + 1]).then_inc(s_exp, 1)

            def evacuate(tile, t, j):
                g, b, hh = tile_of(t)
                wait(act, s_tr, 4 * tile + j + 1)
                nc.scalar.activation(pt[:, hh, 4 * j:4 * j + 4, b * P:(b + 1) * P],
                                     trp[:, j % 2, :].rearrange("p (k q) -> p k q", k=4), ACT.Copy)\
                    .then_inc(s_eva, 1)

            def copy_rden(u, n):
                wait(act, s_ms, u + 1)
                wait(act, s_ctx, n)
                nc.scalar.activation(rdT[:, :], ms[:, 0:QB], ACT.Copy).then_inc(s_mse, 1)

            def turned(u):
                wait(act, s_ms, u + 1)
                nc.scalar.activation(hT[:, :, :], ms[:, :].rearrange("p (c q) -> p c q", c=C), ACT.Copy)\
                    .then_inc(s_mse, 1)

            def relu(u, m0):
                wait(act, s_ms, u + 1)
                for i in range(2):
                    r = nc.scalar.activation(reluT[:, (m0 + i) % (MC // 2), :], ms[:, i * QB:(i + 1) * QB],
                                             ACT.Relu, bias=b1[:, m0 + i:m0 + i + 1])
                r.then_inc(s_mse, 1)

            def tail_step(t, of, base, rden):
                if t == 4:
                    turned(base + 1)
                elif t == 5:
                    relu(base + 2, 0)
                elif t == 6:
                    relu(base + 3, 2)
                elif t == 10:
                    relu(base + rden + 5, 4)
                elif t == 11:
                    relu(base + rden + 6, 6)

            exponentiate(0, 0)

            def body(sb, tail, end, last):
                for t in range(TPB):
                    tile = TPB * sb + t
                    nxt = (tile + 1, (t + 1) % TPB)
                    ahead = not (last and t + 1 >= TPB)
                    g = RDEN.get((t - 1, 3))
                    if g is not None and (g == 0 or tail):
                        copy_rden(rden_use(sb, g, tail), G * sb - g)
                    if tail:
                        tail_step(t, sb - 1, misc_base(sb), 1)
                    evacuate(tile, t, 0)
                    if ahead:
                        exponentiate(*nxt)
                    if end and t == 0:
                        turned(misc_base(sb) - 3)
                    for j in (2, 3):
                        evacuate(tile, t, j)

            def tail_alone(sb):
                turned(misc_base(sb) - 3)
                copy_rden(rden_use(sb, 1, True), G * sb - 1)
                for t in range(TPB):
                    tail_step(t, sb - 1, misc_base(sb), 0)
                turned(misc_base(sb) + 8)

            looped(act, body, tail_alone)


def layer1(nc, a, sem, sbuf, psum, ident, mhalf, whx, x1_dram, out):
    sc, trp, cx, ms = psum
    MC = HID // P
    banks = [sc[:, 0, 0:W], sc[:, 0, W:2 * W], sc[:, 1, 0:W], sc[:, 1, W:2 * W]]
    pair = [ms, cx]
    with ExitStack() as ctx:
        fdb = sbuf(ctx, "f_dst_rows", [P, N])
        fs2 = sbuf(ctx, "f_src_low", [P, KC])
        x1 = sbuf(ctx, "x1_rows", [P, KC, D])
        pb = sbuf(ctx, "probs_l1", [P, 3, N])
        low = sbuf(ctx, "leaky_low", [P, 2, N])
        msk = sbuf(ctx, "mask_l1", [P, N], BF16)
        adj = sbuf(ctx, "adj_l1", [P, 2, N], I32)
        pt = sbuf(ctx, "probs_T_l1", [P, 2, KC, SQ])
        fc = sbuf(ctx, "fc4", [P, D])
        fc1 = sbuf(ctx, "fc1", [P, C, HID])
        fc2 = sbuf(ctx, "fc2", [P, MC, D])
        fb1 = sbuf(ctx, "fc1_b", [P, MC])
        rows = {n: sbuf(ctx, "l1_" + n, [P, D]) for n in ("fc_b", "g", "b", "fc2_b")}
        hp = sbuf(ctx, "h_prime_T", [P, SQ])
        h2 = sbuf(ctx, "h2", [P, ST, D])
        h2T = sbuf(ctx, "h2_T", [P, C, SQ])
        geluT = sbuf(ctx, "gelu_T", [P, MC, SQ])
        yo = sbuf(ctx, "out_rows", [P, ST, D])
        nmax = sbuf(ctx, "neg_max_l1", [P, KC])
        rs = sbuf(ctx, "row_sum_l1", [P, KC])
        rd = sbuf(ctx, "rden_l1", [P, KC])
        st = sbuf(ctx, "stats_l1", [P, ST, 6])
        mv = sbuf(ctx, "mv_l1", [P, ST, 2])
        ve = sbuf(ctx, "rstd_l1", [P, ST])

        s_w, s_x = sem("s_l1_weights"), sem("s_l1_x1")
        NWT = 11
        s_adj = [sem(f"s_l1_adj{i}") for i in range(2)]
        s_fdt, s_fdb, s_fs = sem("s_l1_fd_turned"), sem("s_l1_fd"), sem("s_l1_fs_low")
        s_cv, s_low, s_lr, s_max, s_exp = (sem("s_l1_" + n) for n in ("mask", "low", "leaky", "max", "exp"))
        s_tr, s_eva, s_evd = (sem("s_l1_" + n) for n in ("turned", "evac_act", "evac_dve"))
        s_pv, s_hp, s_fc, s_x2, s_rd = (sem("s_l1_" + n) for n in ("pv", "h_prime", "fc", "x2", "rden"))
        s_xb, s_bn, s_ag, s_ve, s_rstd = (sem("s_l1_" + n) for n in ("x1b", "bn", "aggr", "ve", "rstd"))
        s_nrm, s_g, s_gb, s_ht, s_hte = (sem("s_l1_" + n) for n in ("norm", "gain", "ln", "h2_turned", "h2T"))
        s_up, s_ge, s_dn, s_yc, s_y = (sem("s_l1_" + n) for n in ("up", "gelu", "down", "y_copied", "y"))
        s_x2b, s_out = sem("s_l1_x2b"), sem("s_l1_out")

        block = ctx.enter_context(nc.Block())

        def steps():
            for t in range(KC + 2 * ST):
                s = t // ST
                u = s - 1 if 0 < s <= NS else None
                w = s - 2 if s > 1 else None
                yield t, t % ST, u, w

        @block.sync
        def _(sp):
            def load_adj(t):
                wait(sp, s_cv, t - 1)
                sp.dma_start(adj[:, t % 2, :], a["adj"][t * P:(t + 1) * P, :]).then_inc(s_adj[t % 2], 16)

            load_adj(0)
            load_adj(1)
            sp.dma_start(x1[:, :, :], x1_dram.rearrange("(t p) d -> p t d", p=P)).then_inc(s_x, 16)
            load_adj(2)
            for i in range(4):
                sp.dma_start(fc[DK * i:DK * i + DK, :], a["L1_gnn_fc_wT"]).then_inc(s_w, 16)
            sp.dma_start(rows["fc_b"][:, :], a["L1_gnn_fc_b"].partition_broadcast(P)).then_inc(s_w, 16)
            sp.dma_start(rows["g"][:, :], a["L1_gnn_ln2_g"].partition_broadcast(P)).then_inc(s_w, 16)
            sp.dma_start(rows["b"][:, :], a["L1_gnn_ln2_b"].partition_broadcast(P)).then_inc(s_w, 16)
            sp.dma_start(rows["fc2_b"][:, :], a["L1_gnn_fc2_b"].partition_broadcast(P)).then_inc(s_w, 16)
            sp.dma_start(fc1[:, :, :], a["L1_gnn_fc1_wT"].rearrange("(c p) m -> p c m", p=P)).then_inc(s_w, 16)
            sp.dma_start(fc2[:, :, :], a["L1_gnn_fc2_wT"].rearrange("(c p) m -> p c m", p=P)).then_inc(s_w, 16)
            sp.dma_start(fb1[:, :], a["L1_gnn_fc1_b_cols"]).then_inc(s_w, 16)
            for t in range(3, KC):
                load_adj(t)
            for w in range(NS):
                sp.wait_ge(s_y, w + 1)
                sp.dma_start(out[w * SQ:(w + 1) * SQ, :].rearrange("(t p) d -> p t d", p=P), yo[:, :, :])\
                    .then_inc(s_out, 16)
            sp.wait_ge(s_out, 16 * NS)

        @block.gpsimd
        def _(pool):
            def add_row(s, name, done):
                for i in range(ST):
                    t = s * ST + i
                    add = nc.gpsimd.tensor_tensor(x1[:, t, :], x1[:, t, :], rows[name][:, :], ALU.add)
                add.then_inc(done, 1)

            def layernorm(u):
                wait(pool, s_ag, ST * (u + 1))
                nc.gpsimd.tensor_scalar(ve[:, :], mv[:, :, 1], EPS, None, ALU.add).then_inc(s_ve, 1)
                wait(pool, s_ve, u + 1)
                nc.gpsimd.tensor_tensor(ve[:, :], ve[:, :], mhalf[:, 0:ST], ALU.pow).then_inc(s_rstd, 1)
                wait(pool, s_rstd, u + 1)
                wait(pool, s_ht, u)
                for i in range(ST):
                    nc.gpsimd.tensor_scalar(h2[:, i, :], x1[:, u * ST + i, :], mv[:, i, 0:1], ve[:, i:i + 1],
                                            ALU.subtract, ALU.mult).then_inc(s_nrm, 1)
                for i in range(ST):
                    wait(pool, s_nrm, ST * u + i + 1)
                    nc.gpsimd.tensor_tensor(h2[:, i, :], h2[:, i, :], rows["g"][:, :], ALU.mult).then_inc(s_g, 1)
                for i in range(ST):
                    wait(pool, s_g, ST * u + i + 1)
                    nc.gpsimd.tensor_tensor(h2[:, i, :], h2[:, i, :], rows["b"][:, :], ALU.add).then_inc(s_gb, 1)

            def add_residual(w):
                wait(pool, s_x2b, w + 1)
                wait(pool, s_yc, 2 * (w + 1))
                for i in range(ST):
                    add = nc.gpsimd.tensor_tensor(yo[:, i, :], yo[:, i, :], x1[:, w * ST + i, :], ALU.add)
                add.then_inc(s_y, 1)

            nc.gpsimd.tensor_scalar(fs2[:, :], whx[:, :, DK], 0.2, None, ALU.mult).then_inc(s_fs, 1)
            pool.wait_ge(s_w, 16 * NWT)
            pool.wait_ge(s_x, 16)
            add_row(0, "fc_b", s_xb)
            for s in range(NS + 2):
                if s + 1 < NS:
                    add_row(s + 1, "fc_b", s_xb)
                if 0 < s <= NS:
                    layernorm(s - 1)
                    add_row(s - 1, "fc2_b", s_x2b)
                if s > 1:
                    add_residual(s - 2)

        @block.tensor
        def _(pe):
            def transposes(t, j):
                if j == 0:
                    wait(pe, s_exp, t + 1)
                if j == 3:
                    wait(pe, s_evd, t + 1)
                else:
                    wait(pe, s_eva, 3 * t + j - 1)
                for m in range(4):
                    k = 4 * j + m
                    mm = nc.tensor.transpose(trp[:, j % 2, m * P:(m + 1) * P], pb[:, t % 3, k * P:(k + 1) * P],
                                             ident[:, :])
                mm.then_inc(s_tr, 1)

            def pv(u):
                wait(pe, s_eva, 3 * ST * (u + 1))
                wait(pe, s_evd, ST * (u + 1))
                wait(pe, s_yc, 2 * (u - 1))
                for k in range(KC):
                    c = k % 4
                    mm = nc.tensor.matmul(cx[DK * c:DK * c + DK, :], whx[:, k, 0:DK], pt[:, u % 2, k, :],
                                          start=(k < 4), stop=(k >= KC - 4))
                mm.then_inc(s_pv, 1)

            def project(u):
                pe.wait_ge(s_w, 16 * NWT)
                wait(pe, s_hp, u + 1)
                wait(pe, s_yc, 2 * (u - 1))
                for m in range(ST):
                    mm = nc.tensor.matmul(pair[m // 2][:, (m % 2) * D:(m % 2 + 1) * D], hp[:, m * P:(m + 1) * P],
                                          fc[:, :], start=True, stop=True)
                    mm.then_inc(s_fc, 1)

            def turn_h2(u):
                wait(pe, s_gb, ST * (u + 1))
                wait(pe, s_ge, MC * u)
                for c in range(C):
                    for i in range(ST):
                        mm = nc.tensor.transpose(banks[c][:, i * P:(i + 1) * P], h2[:, i, c * P:(c + 1) * P],
                                                 ident[:, :])
                mm.then_inc(s_ht, 1)

            def up(w, m):
                wait(pe, s_hte, C * (w + 1))
                wait(pe, s_ge, MC * w)
                for c in range(C):
                    mm = nc.tensor.matmul(banks[m], fc1[:, c, m * P:(m + 1) * P], h2T[:, c, :],
                                          start=(c == 0), stop=(c == C - 1))
                mm.then_inc(s_up, 1)

            def down(w, i):
                wait(pe, s_ge, MC * (w + 1))
                wait(pe, s_x2, ST * min(w + 2, NS))
                for m in range(MC):
                    mm = nc.tensor.matmul(pair[i // 2][:, (i % 2) * D:(i % 2 + 1) * D],
                                          geluT[:, m, i * P:(i + 1) * P], fc2[:, m, :],
                                          start=(m == 0), stop=(m == MC - 1))
                mm.then_inc(s_dn, 1)

            for k in range(KC):
                mm = nc.tensor.transpose(banks[k // 4][:, (k % 4) * P:(k % 4 + 1) * P],
                                         whx[:, k, DK + 1:DK + 2].to_broadcast([P, P]), ident[:, :])
                if k % 4 == 3:
                    mm.then_inc(s_fdt, 1)

            for t, r, u, w in steps():
                for j in range(4):
                    if t < KC:
                        transposes(t, j)
                    if w is not None:
                        if (r, j) in UP:
                            up(w, UP[r, j])
                        if (r, j) in DOWN:
                            down(w, DOWN[r, j])
                    if u is not None:
                        if (r, j) == (0, 1):
                            pv(u)
                        elif (r, j) == (1, 1):
                            project(u)
                        elif (r, j) == (3, 3):
                            turn_h2(u)

        @block.scalar
        def _(act):
            def exponentiate(t):
                wait(act, s_max, t + 1)
                nc.scalar.activation(pb[:, t % 3, :], pb[:, t % 3, :], ACT.Exp, bias=nmax[:, t:t + 1], scale=-1.0,
                                     accum_out=rs[:, t:t + 1]).then_inc(s_exp, 1)

            def leaky_low(t):
                wait(act, s_lr, t - 1)
                nc.scalar.activation(low[:, t % 2, :], fdb[:, :], ACT.Identity, bias=fs2[:, t:t + 1], scale=0.2)\
                    .then_inc(s_low, 1)

            def evacuate(t, j):
                wait(act, s_tr, 4 * t + j + 1)
                if t % ST == 0:
                    wait(act, s_pv, t // ST - 1)
                nc.scalar.activation(pt[:, (t // ST) % 2, 4 * j:4 * j + 4, (t % ST) * P:(t % ST + 1) * P],
                                     trp[:, j % 2, :].rearrange("p (k q) -> p k q", k=4), ACT.Copy)\
                    .then_inc(s_eva, 1)

            for j in range(4):
                act.wait_ge(s_fdt, j + 1)
                nc.scalar.activation(fdb[:, j * W:(j + 1) * W], banks[j], ACT.Copy).then_inc(s_fdb, 1)
            act.wait_ge(s_fs, 1)
            act.wait_ge(s_fdb, 4)
            leaky_low(0)
            leaky_low(1)
            exponentiate(0)
            leaky_low(2)
            for t, r, u, w in steps():
                if t < KC:
                    evacuate(t, 0)
                if t + 1 < KC:
                    exponentiate(t + 1)
                if t < KC:
                    evacuate(t, 2)
                    evacuate(t, 3)
                if u is not None and r == 0:
                    wait(act, s_pv, u + 1)
                    wait(act, s_fc, ST * u)
                    nc.scalar.activation(hp[:, :], cx[:, :], ACT.Copy).then_inc(s_hp, 1)
                if w is not None and r == 1:
                    act.wait_ge(s_w, 16 * NWT)
                    wait(act, s_dn, ST * w)
                    wait(act, s_up, MC * (w + 1))
                    for m in range(MC):
                        nc.scalar.activation(geluT[:, m, :], banks[m], ACT.Gelu, bias=fb1[:, m:m + 1])\
                            .then_inc(s_ge, 1)
                if w is not None and r == 3:
                    wait(act, s_out, 16 * w)
                    for i in range(2):
                        wait(act, s_dn, ST * w + 2 * i + 2)
                        nc.scalar.activation(yo[:, 2 * i:2 * i + 2, :],
                                             pair[i][:, :].rearrange("p (b d) -> p b d", b=2), ACT.Copy)\
                            .then_inc(s_yc, 1)
                if u is not None and r == 3:
                    wait(act, s_ht, u + 1)
                    wait(act, s_up, MC * u)
                    for c in range(C):
                        nc.scalar.activation(h2T[:, c, :], banks[c], ACT.Copy).then_inc(s_hte, 1)
                if t + 3 < KC:
                    leaky_low(t + 3)

        @block.vector
        def _(dve):
            def leaky(t):
                wait(dve, s_low, t + 1)
                wait(dve, s_tr, 4 * (t - 2))
                nc.vector.scalar_tensor_tensor(out=pb[:, t % 3, :], in0=fdb[:, :], scalar=whx[:, t, DK:DK + 1],
                                               in1=low[:, t % 2, :], op0=ALU.add, op1=ALU.max).then_inc(s_lr, 1)

            def mask(t):
                wait(dve, s_adj[t % 2], 16 * (t // 2 + 1))
                wait(dve, s_max, t)
                nc.vector.tensor_scalar(msk[:, :], adj[:, t % 2, :], 0, NEG, ALU.is_le, ALU.mult).then_inc(s_cv, 1)

            def reduce(t):
                wait(dve, s_lr, t + 1)
                wait(dve, s_cv, t + 1)
                nc.vector.tensor_tensor_reduce(out=pb[:, t % 3, :], in0=pb[:, t % 3, :], in1=msk[:, :],
                                               scale=-1.0, scalar=BIG, op0=ALU.add, op1=ALU.min,
                                               accum_out=nmax[:, t:t + 1]).then_inc(s_max, 1)

            def residual(u):
                wait(dve, s_exp, ST * (u + 1))
                nc.vector.reciprocal(rd[:, u * ST:(u + 1) * ST], rs[:, u * ST:(u + 1) * ST]).then_inc(s_rd, 1)
                wait(dve, s_rd, u + 1)
                wait(dve, s_xb, u + 1)
                for i in range(ST):
                    t = u * ST + i
                    wait(dve, s_fc, u * ST + 2 * (i // 2) + 2)
                    nc.vector.scalar_tensor_tensor(out=x1[:, t, :], in0=pair[i // 2][:, (i % 2) * D:(i % 2 + 1) * D],
                                                   scalar=rd[:, t:t + 1], in1=x1[:, t, :], op0=ALU.mult,
                                                   op1=ALU.add).then_inc(s_x2, 1)
                for i in range(ST):
                    wait(dve, s_x2, ST * u + i + 1)
                    nc.vector.bn_stats(st[:, i, :], x1[:, u * ST + i, :]).then_inc(s_bn, 1)
                wait(dve, s_nrm, ST * u)
                for i in range(ST):
                    wait(dve, s_bn, ST * u + i + 1)
                    nc.vector.bn_aggr(mv[:, i, :], st[:, i, :]).then_inc(s_ag, 1)

            dve.wait_ge(s_fdb, 4)
            for t in range(2):
                mask(t)
                leaky(t)
                reduce(t)
            for t, r, u, w in steps():
                if t + 2 < KC:
                    mask(t + 2)
                if t < KC:
                    wait(dve, s_tr, 4 * t + 2)
                    if t % ST == 0:
                        wait(dve, s_pv, t // ST - 1)
                    nc.vector.tensor_copy(pt[:, (t // ST) % 2, 4:8, (t % ST) * P:(t % ST + 1) * P],
                                          trp[:, 1, :].rearrange("p (k q) -> p k q", k=4)).then_inc(s_evd, 1)
                if t + 2 < KC:
                    leaky(t + 2)
                    reduce(t + 2)
                if u is not None and r == 1:
                    residual(u)


UP = {(0, 0): 0, (1, 0): 1, (1, 2): 2, (1, 3): 3}
DOWN = {(2, 1): 0, (2, 3): 1, (3, 0): 2, (3, 2): 3}


TRANSPOSED = ("L1_gnn_W", "L0_gnn_Wq", "L0_gnn_Wk", "L0_gnn_Wv", "L0_gnn_Wo", "L0_gnn_W1", "L0_gnn_W2",
              "L1_gnn_fc_w", "L1_gnn_fc1_w", "L1_gnn_fc2_w")
COLUMNS = ("L0_gnn_bq", "L0_gnn_bk", "L0_gnn_b1", "L1_gnn_fc1_b")
AS_IS = ("x", "adj", "L0_gnn_bv", "L0_gnn_bo", "L0_gnn_b2",
         "L0_gnn_ln1_g", "L0_gnn_ln1_b", "L0_gnn_ln2_g", "L0_gnn_ln2_b", "L1_gnn_a",
         "L1_gnn_fc_b", "L1_gnn_ln1_g", "L1_gnn_ln1_b", "L1_gnn_ln2_g", "L1_gnn_ln2_b",
         "L1_gnn_fc2_b")


def kernel(**inputs):
    import concourse.bacc as bacc
    from concourse.bass_utils import run_bass_kernel_spmd

    host = {n: np.ascontiguousarray(inputs[n]) for n in AS_IS}
    host.update({n + "T": np.ascontiguousarray(np.asarray(inputs[n]).T) for n in ("x",) + TRANSPOSED})
    for n in COLUMNS:
        host[n + "_cols"] = np.ascontiguousarray(np.asarray(inputs[n]).reshape(-1, P).T)
    host["ident"] = np.eye(P, dtype=np.float32)
    host["ident_i"] = np.eye(P, dtype=np.int32)
    nc = bacc.Bacc("TRN2", target_bir_lowering=False, num_devices=1)
    aps = {n: nc.dram_tensor(f"in_{n}", x.shape, mybir.dt.from_np(x.dtype), kind="ExternalInput").ap()
           for n, x in host.items()}
    out = nc.dram_tensor("out_rows_dram", (N, D), F32, kind="ExternalOutput").ap()
    build(nc, aps, out)
    r = run_bass_kernel_spmd(nc, [{f"in_{n}": x for n, x in host.items()}], core_ids=[0])
    return r.results[0]["out_rows_dram"]
```
